# Optimizing a Trainium2 kernel written in Bass

```python
import numpy as np
import jax
import jax.numpy as jnp

def _softmax(x, axis=-1):
    return jax.nn.softmax(x, axis=axis)

def _gelu(x):
    return jax.nn.gelu(x, approximate=True)

def _silu(x):
    return jax.nn.silu(x)

def _sigmoid(x):
    return jax.nn.sigmoid(x)

def _layernorm(x, axis=-1, eps=1e-05):
    m = jnp.mean(x, axis=axis, keepdims=True)
    v = jnp.var(x, axis=axis, keepdims=True)
    return (x - m) / jnp.sqrt(v + eps)

def _scatter_add(tgt, idx, src, axis=0):
    return tgt.at[idx].add(src)

def _segment_sum(src, seg, n):
    return jax.ops.segment_sum(src, seg, n)
kernel_name = 'mk_vit_tower_d1_tok_img1024_r4_540a04'

def setup_inputs(seed: int=0):
    np.random.seed(seed)
    _w = jnp.asarray

    def _rec_inputs():
        import jax
        import jax.numpy as jnp
        _rk = jax.random.key(seed)
        x = -0.00150118 + 0.499729 * jax.random.normal(jax.random.fold_in(_rk, 1), (16, 256, 64, 2), jnp.float32)
        return x
    x = _rec_inputs()

    def _L0_tok_setup():
        import jax, jax.numpy as jnp
        import numpy as np
        import math
        H = 256
        N = 64
        CH = 1
        SEQ_L = 256
        key = jax.random.key(seed)
        k1, k2, k3, k4 = jax.random.split(key, 4)
        log_dt = jax.random.uniform(k1, (H,), dtype=jnp.float32, minval=math.log(0.001), maxval=math.log(0.1))
        inv_A_real = jnp.log(0.5 * jnp.ones((H, N), jnp.float32)) + 0.1 * jax.random.normal(k2, (H, N), dtype=jnp.float32)
        A_imag = jnp.broadcast_to(math.pi * jnp.arange(N, dtype=jnp.float32), (H, N)).copy()
        B_ri = jax.random.normal(k3, (H, N, 2), dtype=jnp.float32) * 0.5
        C_ri = jax.random.normal(k4, (CH, H, N, 2), dtype=jnp.float32) * 0.5
        return {'log_dt': log_dt, 'inv_A_real': inv_A_real, 'A_imag': A_imag, 'B_ri': B_ri, 'C_ri': C_ri, 'L': SEQ_L}
    _L0_tok_all = _L0_tok_setup()
    _L0_tok_in = {k: v for k, v in _L0_tok_all.items() if k in ('log_dt', 'inv_A_real', 'A_imag', 'B_ri')}
    del _L0_tok_all

    def _L0_attn_setup():
        import jax, jax.numpy as jnp
        import numpy as np
        EMBED_DIM = 256
        NUM_HEADS = 16
        HEAD_DIM = EMBED_DIM // NUM_HEADS
        key = jax.random.key(seed)
        k_x, k_wq, k_bq, k_wo, k_bo = jax.random.split(key, 5)
        D = EMBED_DIM
        s_in = 1.0 / np.sqrt(D)
        x = jax.random.normal(k_x, (2, 512, D), dtype=jnp.float32)
        W_qkv = jax.random.uniform(k_wq, (D, 3 * D), minval=-s_in, maxval=s_in, dtype=jnp.float32)
        b_qkv = jax.random.uniform(k_bq, (3 * D,), minval=-s_in, maxval=s_in, dtype=jnp.float32)
        W_out = jax.random.uniform(k_wo, (D, D), minval=-s_in, maxval=s_in, dtype=jnp.float32)
        b_out = jax.random.uniform(k_bo, (D,), minval=-s_in, maxval=s_in, dtype=jnp.float32)
        return {'x': x, 'W_qkv': W_qkv, 'b_qkv': b_qkv, 'W_out': W_out, 'b_out': b_out}
    _L0_attn_all = _L0_attn_setup()
    _L0_attn_in = {k: v for k, v in _L0_attn_all.items() if k in ('W_qkv', 'b_qkv', 'W_out', 'b_out')}
    del _L0_attn_all

    def _L0_ffn_setup():
        import jax, jax.numpy as jnp
        import numpy as np
        B, S, D = (1, 512, 256)
        F = 352
        E = 16
        K = 2
        CAP_FACTOR = 1.25

        def _mlp(h, wg, wu, wd):
            return jax.nn.silu(h @ wg) * (h @ wu) @ wd
        key = jax.random.key(seed)
        ks = jax.random.split(key, 10)
        sd = 0.02
        return {'x': jax.random.normal(ks[0], (B, S, D), jnp.float32), 'router_w': jax.random.normal(ks[1], (D, E), jnp.float32) * sd, 'router_b': jnp.zeros((E,), jnp.float32), 'w_gate': jax.random.normal(ks[2], (E, D, F), jnp.float32) * sd, 'w_up': jax.random.normal(ks[3], (E, D, F), jnp.float32) * sd, 'w_down': jax.random.normal(ks[4], (E, F, D), jnp.float32) * sd, 'sw_gate': jax.random.normal(ks[5], (D, F), jnp.float32) * sd, 'sw_up': jax.random.normal(ks[6], (D, F), jnp.float32) * sd, 'sw_down': jax.random.normal(ks[7], (F, D), jnp.float32) * sd}
    _L0_ffn_all = _L0_ffn_setup()
    _L0_ffn_in = {k: v for k, v in _L0_ffn_all.items() if k in ('router_w', 'router_b', 'w_gate', 'w_up', 'w_down', 'sw_gate', 'sw_up', 'sw_down')}
    del _L0_ffn_all
    return {'x': x, 'L0_tok_log_dt': _L0_tok_in['log_dt'], 'L0_tok_inv_A_real': _L0_tok_in['inv_A_real'], 'L0_tok_A_imag': _L0_tok_in['A_imag'], 'L0_tok_B_ri': _L0_tok_in['B_ri'], 'L0_attn_W_qkv': _L0_attn_in['W_qkv'], 'L0_attn_b_qkv': _L0_attn_in['b_qkv'], 'L0_attn_W_out': _L0_attn_in['W_out'], 'L0_attn_b_out': _L0_attn_in['b_out'], 'L0_ffn_router_w': _L0_ffn_in['router_w'], 'L0_ffn_router_b': _L0_ffn_in['router_b'], 'L0_ffn_w_gate': _L0_ffn_in['w_gate'], 'L0_ffn_w_up': _L0_ffn_in['w_up'], 'L0_ffn_w_down': _L0_ffn_in['w_down'], 'L0_ffn_sw_gate': _L0_ffn_in['sw_gate'], 'L0_ffn_sw_up': _L0_ffn_in['sw_up'], 'L0_ffn_sw_down': _L0_ffn_in['sw_down']}

def reference(x, L0_tok_log_dt, L0_tok_inv_A_real, L0_tok_A_imag, L0_tok_B_ri, L0_attn_W_qkv, L0_attn_b_qkv, L0_attn_W_out, L0_attn_b_out, L0_ffn_router_w, L0_ffn_router_b, L0_ffn_w_gate, L0_ffn_w_up, L0_ffn_w_down, L0_ffn_sw_gate, L0_ffn_sw_up, L0_ffn_sw_down):
    import jax
    import jax.numpy as jnp

    def _L0_tok_ref(log_dt, inv_A_real, A_imag, B_ri, C_ri, L):
        import jax, jax.numpy as jnp
        import numpy as np
        import math
        H = 256
        N = 64
        CH = 1
        SEQ_L = 256
        dt = jnp.exp(log_dt)
        A = -jnp.exp(inv_A_real) + 1j * A_imag
        B = B_ri[..., 0] + 1j * B_ri[..., 1]
        C = C_ri[..., 0] + 1j * C_ri[..., 1]
        dtA = A * dt[:, None]
        dA = (1.0 + dtA / 2) / (1.0 - dtA / 2)
        C_term = C * B[None]
        log_dA = jnp.log(dA)
        V = jnp.exp(log_dA[:, :, None] * jnp.arange(L))
        K = 2.0 * jnp.einsum('chn,hnl->chl', C_term, V).real
        return K.astype(jnp.float32)

    def _L0_attn_ref(x, W_qkv, b_qkv, W_out, b_out):
        import jax, jax.numpy as jnp
        import numpy as np
        EMBED_DIM = 256
        NUM_HEADS = 16
        HEAD_DIM = EMBED_DIM // NUM_HEADS
        B, N, D = x.shape
        H, Dh = (NUM_HEADS, HEAD_DIM)
        qkv = x @ W_qkv + b_qkv
        qkv = qkv.reshape(B, N, 3, H, Dh)
        q = qkv[:, :, 0].transpose(0, 2, 1, 3)
        k = qkv[:, :, 1].transpose(0, 2, 1, 3)
        v = qkv[:, :, 2].transpose(0, 2, 1, 3)
        scale = 1.0 / jnp.sqrt(jnp.float32(Dh)).astype(x.dtype)
        scores = jnp.einsum('bhqd,bhkd->bhqk', q, k) * scale
        attn = jax.nn.softmax(scores, axis=-1)
        out = jnp.einsum('bhqk,bhkd->bhqd', attn, v)
        out = out.transpose(0, 2, 1, 3).reshape(B, N, D)
        return out @ W_out + b_out

    def _L0_ffn_ref(x, router_w, router_b, w_gate, w_up, w_down, sw_gate, sw_up, sw_down):
        import jax, jax.numpy as jnp
        import numpy as np
        B, S, D = (1, 512, 256)
        F = 352
        E = 16
        K = 2
        CAP_FACTOR = 1.25

        def _mlp(h, wg, wu, wd):
            return jax.nn.silu(h @ wg) * (h @ wu) @ wd
        b, s, d = x.shape
        N = b * s
        NK = N * K
        C = int(np.ceil(CAP_FACTOR * NK / E))
        x_tokens = x.reshape(N, d)
        logits = x_tokens @ router_w + router_b
        probs = jax.nn.softmax(logits, axis=-1)
        vals, idx = jax.lax.top_k(probs, K)
        vals = vals / (jnp.sum(vals, axis=-1, keepdims=True) + 1e-09)
        idx_flat = idx.reshape(NK)
        vals_flat = vals.reshape(NK)
        oh_e = jax.nn.one_hot(idx_flat, E, dtype=x.dtype)
        pos = (jnp.cumsum(oh_e, axis=0) * oh_e).sum(axis=1) - 1
        within = (pos < C).astype(x.dtype)
        pos_c = jnp.clip(pos, 0, C - 1).astype(jnp.int32)
        token_ids = jnp.arange(NK) // K
        x_pair = x_tokens[token_ids] * within[:, None]
        expert_inputs = jnp.zeros((E, C, d), x.dtype).at[idx_flat, pos_c].add(x_pair)
        expert_outputs = jax.vmap(_mlp)(expert_inputs, w_gate, w_up, w_down)
        gathered = expert_outputs[idx_flat, pos_c] * (vals_flat * within)[:, None]
        output_tokens = gathered.reshape(N, K, d).sum(axis=1)
        return x + _mlp(x, sw_gate, sw_up, sw_down) + output_tokens.reshape(b, s, d)
    h = _L0_tok_ref(L0_tok_log_dt, L0_tok_inv_A_real, L0_tok_A_imag, L0_tok_B_ri, x, 256)
    h = h + _L0_attn_ref(_layernorm(h, axis=-1), L0_attn_W_qkv, L0_attn_b_qkv, L0_attn_W_out, L0_attn_b_out)
    h = h + _L0_ffn_ref(_layernorm(h, axis=-1), L0_ffn_router_w, L0_ffn_router_b, L0_ffn_w_gate, L0_ffn_w_up, L0_ffn_w_down, L0_ffn_sw_gate, L0_ffn_sw_up, L0_ffn_sw_down)
    return h

_drawn_inputs = setup_inputs


def setup_inputs(seed=0):
    import zlib

    import numpy as np

    out = dict(_drawn_inputs(seed))
    spreads = {'L0_ffn_router_b': (0.0, 0.8)}
    factors = {'L0_attn_W_qkv': 8.0,
     'L0_attn_b_qkv': 8.0,
     'L0_attn_W_out': 7.52,
     'L0_attn_b_out': 6.63,
     'L0_ffn_router_w': 8.0,
     'L0_ffn_w_gate': 8.0,
     'L0_ffn_w_up': 8.0,
     'L0_ffn_w_down': 8.0,
     'L0_ffn_sw_gate': 8.0,
     'L0_ffn_sw_up': 8.0,
     'L0_ffn_sw_down': 8.0}
    for name, (base, spread) in spreads.items():
        noise = np.random.default_rng([zlib.crc32(name.encode()), seed]).standard_normal(out[name].shape)
        drawn = base * np.exp(spread * noise) if base else spread * noise
        out[name] = jnp.asarray(drawn.astype(out[name].dtype))
    for name, factor in factors.items():
        out[name] = (out[name] * factor).astype(out[name].dtype)
    return out
```

```python
import math
from contextlib import ExitStack

import concourse.bass as bass
from concourse import mybir

ALU = mybir.AluOpType
ACT = mybir.ActivationFunctionType
AX = mybir.AxisListType
F32 = mybir.dt.float32
F32R = mybir.dt.float32r
I32 = mybir.dt.int32
U32 = mybir.dt.uint32

P = 128


class Chain:

    def __init__(self, eng, sem):
        self.eng, self.sem, self.base, self.k = eng, sem, 0, 0

    def link(self, ins):
        self.k += 1
        ins.then_inc(self.sem, 1)
        self.eng.wait_ge(self.sem, self.base + self.k)

    def tick(self, ins):
        self.k += 1
        ins.then_inc(self.sem, 1)

    def start(self, base):
        self.base, self.k = base, 0


def rolled(eng, span, step, chain=None):
    first, lo, hi, last = span
    per = 0

    def written_out(steps):
        nonlocal per
        for n in steps:
            if chain:
                chain.start(chain.base + chain.k)
            step(n, n % 2, n // 2)
            per = chain.k if chain else 0

    written_out(range(first, lo))
    base = chain.base + chain.k if chain else 0
    if lo == hi:
        return written_out(range(hi, last))
    with eng.Fori(lo // 2, hi // 2) as i:
        for b in range(2):
            if chain:
                chain.start(base + per * (2 * i + b - lo))
            step(2 * i + b, b, i)
            assert not chain or chain.k == per
    if chain:
        chain.start(base + per * (hi - lo))
    written_out(range(hi, last))


def make_tokens(nc, x, log_dt, inv_A_real, A_imag, B_ri, ident, psum, h_dram):
    C, S, N, _ = x.shape
    J = S // 2
    GP = 16
    NG = J // GP
    LB = 128
    A = 2
    QG = GP // 2
    KP = 8
    SPLIT = 12
    NCB = C // 2
    TT = nc.vector.tensor_tensor

    with ExitStack() as ctx:
        def sb(name, shape, dt=F32):
            return ctx.enter_context(nc.sbuf_tensor(name, shape, dt))

        def sem(name):
            return ctx.enter_context(nc.semaphore(name))

        x_rows = sb("x_rows", [P, C, 256])
        ldt = sb("ldt", [P, 2])
        dt = sb("dt", [P, 2])
        a_raw = sb("a_raw", [P, P])
        a_exp = sb("a_exp", [P, P])
        e_base = sb("e_base", [P, 2])
        a_im = sb("a_im", [P, P])
        b_rows = sb("b_rows", [P, 256])
        wr = sb("wr", [P, P])
        wi = sb("wi", [P, P])
        tmp = sb("tmp", [P, 6, P])
        z_rows = sb("z_rows", [P, KP, 2, P])
        z_re = sb("z_re", [P, KP, J])
        z_im = sb("z_im", [P, KP, 2, J])
        b_re = sb("b_re", [P, J])
        b_im = sb("b_im", [P, 2, J])
        c_t = sb("c_t", [P, 2, C, J])
        g_cmp = sb("g_cmp", [P, 2, A, 2, C, GP])
        g_t = sb("g_t", [P, 2, C, GP])
        g_u = sb("g_u", [P, 2, C, GP])
        g_blk = sb("g_blk", [P, 2, 2, GP, 2, A, C])
        w_pow = sb("w_pow", [P, 2, 2, GP, LB])
        w_t = sb("w_t", [P, 2, GP, LB // 2])
        w_u = sb("w_u", [P, 2, GP, LB // 2])
        h_out = sb("h_out", [P, 2, 2, 512])

        ident_ready = sem("ident_ready")
        par_loaded = sem("par_loaded")
        x_loaded = sem("x_loaded")
        exp_ready = sem("exp_ready")
        dve_chain = sem("dve_chain1")
        pool_chain = sem("pool_chain1")
        z_ready = sem("z_ready")
        tr_ready = sem("tr_ready")
        tr_copied = sem("tr_copied")
        const_ready = sem("const_ready")
        g_ready = sem("g_ready")
        blk_ready = sem("blk_ready")
        w_low = sem("w_low")
        w_dve = sem("w_dve")
        w_pool = sem("w_pool")
        prod_ready = sem("prod_ready")
        out_ready = sem("out_ready")
        stored = [sem(f"stored{b}") for b in range(2)]

        x_v = x.rearrange("c (j s) n r -> j c (s n r)", s=2)
        h_v = h_dram.rearrange("c (q j s) (a b) -> j s a c q b", j=2, s=2, a=A)
        TR_C, TR_Z = NCB, NCB + 1 + KP // 2
        CP_C, CP_B = NCB, NCB + 3

        block = ctx.enter_context(nc.Block())

        @block.sync
        def _(sp):
            sp.dma_start(ldt[:], log_dt.rearrange("(j s) -> j s", s=2)).then_inc(par_loaded, 16)
            sp.dma_start(a_raw[:], inv_A_real.rearrange("(j s) n -> j (s n)", s=2)).then_inc(par_loaded, 16)
            sp.dma_start(a_im[:], A_imag.rearrange("(j s) n -> j (s n)", s=2)).then_inc(par_loaded, 16)
            sp.dma_start(b_rows[:], B_ri.rearrange("(j s) n r -> j (s n r)", s=2)).then_inc(par_loaded, 16)
            for k in range(4):
                sp.dma_start(x_rows[:, 4 * k:4 * k + 4], x_v[:, 4 * k:4 * k + 4]).then_inc(x_loaded, 16)

            def store(g, b, i):
                sp.wait_ge(out_ready, 2 * g + 2)
                for j in range(2):
                    for s in range(2):
                        for a in range(A):
                            p0 = 64 * j + 32 * s + 16 * a
                            sp.dma_start(h_v[j, s, a][:, bass.ts(g, QG), :],
                                         h_out[p0:p0 + C, b].rearrange("c k (q b) -> c (k q) b", b=LB)
                                         ).then_inc(stored[b], 16)

            rolled(sp, (0, 0, NG, NG), store)
            for b in range(2):
                sp.wait_ge(stored[b], 64 * NG)

        @block.scalar
        def _(act):
            act.wait_ge(par_loaded, 64)
            nc.scalar.activation(a_exp[:], a_raw[:], ACT.Exp).then_inc(exp_ready, 1)
            for n in range(NCB):
                act.wait_ge(tr_ready, n + 1)
                nc.scalar.activation(c_t[:, :, 2 * n:2 * n + 2, :].rearrange("p r c j -> p c r j"),
                                     psum[n % 4][:].rearrange("p (c r j) -> p c r j", c=2, r=2),
                                     ACT.Copy).then_inc(tr_copied, 1)
            act.wait_ge(tr_ready, NCB + 1)
            bank = psum[NCB % 4]
            nc.scalar.activation(b_re[:], bank[:, 0:J], ACT.Copy, scale=2.0).then_inc(tr_copied, 1)
            nc.scalar.activation(b_im[:, 0], bank[:, J:2 * J], ACT.Copy, scale=2.0).then_inc(tr_copied, 1)
            nc.scalar.activation(b_im[:, 1], bank[:, J:2 * J], ACT.Copy, scale=-2.0).then_inc(tr_copied, 1)
            for q in range(KP // 2):
                act.wait_ge(tr_ready, NCB + 2 + q)
                v = psum[(NCB + 1 + q) % 4][:].rearrange("p (k r j) -> p k r j", k=2, r=2)
                k2 = slice(2 * q, 2 * q + 2)
                nc.scalar.activation(z_re[:, k2], v[:, :, 0], ACT.Copy).then_inc(tr_copied, 1)
                nc.scalar.activation(z_im[:, k2, 0], v[:, :, 1], ACT.Copy).then_inc(tr_copied, 1)
                nc.scalar.activation(z_im[:, k2, 1], v[:, :, 1], ACT.Copy, scale=-1.0).then_inc(tr_copied, 1)
            act.wait_ge(const_ready, 3)

            def lay_out(g, b):
                act.wait_ge(g_ready, 2 * g + 2)
                if not (isinstance(g, int) and g < 2):
                    act.wait_ge(prod_ready, g - 1)
                for r in range(2):
                    for s in range(2):
                        src = g_cmp[64 * s:64 * s + 64, b, :, r].rearrange("p a c j -> p j a c")
                        nc.scalar.activation(g_blk[64 * s:64 * s + 64, b, r, :, s], src, ACT.Copy,
                                             scale=-1.0 if r else 1.0).then_inc(blk_ready, 1)

            def copy_out(g, b, i):
                act.wait_ge(prod_ready, g + 1)
                if not (isinstance(g, int) and g < 2):
                    act.wait_ge(stored[b], 128 * i)
                for k in range(2):
                    nc.scalar.activation(h_out[:, b, k], psum[2 * b + k][:], ACT.Copy).then_inc(out_ready, 1)

            def step(n, b, i):
                lay_out(n, b)
                if not (isinstance(n, int) and n < 1):
                    copy_out(n - 1, 1 - b, i + b - 1)

            rolled(act, (0, 2, NG, NG), step)
            copy_out(NG - 1, (NG - 1) % 2, (NG - 1) // 2)

        @block.vector
        def _(dve):
            ch = Chain(dve, dve_chain)
            link = ch.link
            nc.vector.memset(w_pow[:, :, 0, :, 0:1], 1.0).then_inc(const_ready, 1)
            nc.vector.memset(w_pow[:, :, 1, :, 0:1], 0.0).then_inc(const_ready, 1)
            dve.wait_ge(exp_ready, 2)
            for s in range(2):
                h = slice(64 * s, 64 * s + 64)
                nc.vector.tensor_scalar(wr[:, h], a_exp[:, h], dt[:, s:s + 1], -0.5, ALU.mult,
                                        ALU.mult).then_inc(dve_chain, 1)
                nc.vector.tensor_scalar(wi[:, h], a_im[:, h], dt[:, s:s + 1], 0.5, ALU.mult,
                                        ALU.mult).then_inc(dve_chain, 1)
            ch.k = 4
            dve.wait_ge(dve_chain, 4)
            t = [tmp[:, i] for i in range(6)]
            zr, zi = z_rows[:, 0, 0], z_rows[:, 0, 1]
            link(nc.vector.tensor_scalar(t[0], wr[:], -1.0, 1.0, ALU.mult, ALU.add))
            link(nc.vector.tensor_scalar(t[1], wr[:], 1.0, None, ALU.add))
            link(TT(t[2], wi[:], wi[:], ALU.mult))
            link(TT(t[1], t[0], t[1], ALU.mult))
            link(TT(t[3], t[0], t[0], ALU.mult))
            link(TT(t[3], t[3], t[2], ALU.add))
            link(nc.vector.reciprocal(t[4], t[3]))
            link(TT(t[1], t[1], t[2], ALU.subtract))
            link(TT(zr, t[1], t[4], ALU.mult))
            link(nc.vector.scalar_tensor_tensor(out=zi, in0=wi[:], scalar=2.0, in1=t[4], op0=ALU.mult, op1=ALU.mult))
            for k in range(1, KP):
                r0, i0 = z_rows[:, k - 1, 0], z_rows[:, k - 1, 1]
                link(TT(t[0], r0, r0, ALU.mult))
                link(TT(t[1], i0, i0, ALU.mult))
                link(nc.vector.scalar_tensor_tensor(out=z_rows[:, k, 1], in0=r0, scalar=2.0, in1=i0,
                                                    op0=ALU.mult, op1=ALU.mult))
                last = TT(z_rows[:, k, 0], t[0], t[1], ALU.subtract)
                link(last)
                if k % 2:
                    dve.nop().then_inc(z_ready, 1)
            dve.wait_ge(tr_copied, CP_B + 3 * (KP // 2))

            def step(g, b, i):
                if not (isinstance(g, int) and g < 2):
                    dve.wait_ge(prod_ready, g - 1)
                js = bass.ts(g, GP)
                w = w_pow[:, b]
                link(nc.vector.tensor_copy(w[:, 0, :, 1], z_re[:, 0, js]))
                link(nc.vector.tensor_copy(w[:, 1, :, 1], z_im[:, 0, 0, js]))
                for k in range(1, KP - 1):
                    m = 1 << k
                    n = SPLIT if k == KP - 2 else GP
                    if k == KP - 2:
                        dve.nop().then_inc(w_low, 1)
                    jn = bass.ds(g * GP, n)
                    zr = z_re[:, k, jn].unsqueeze(1).unsqueeze(3).to_broadcast([P, 2, n, m])
                    zi = z_im[:, k, :, jn].unsqueeze(3).to_broadcast([P, 2, n, m])
                    wt, wu = w_t[:, :, 0:n, 0:m], w_u[:, :, 0:n, 0:m]
                    link(TT(wt, w[:, :, 0:n, 0:m], zr, ALU.mult))
                    link(TT(wu, w[:, :, 0:n, 0:m], zi, ALU.mult))
                    link(TT(w[:, :, 0:n, m:2 * m], wt, w_u[:, ::-1, 0:n, 0:m], ALU.add))
                dve.nop().then_inc(w_dve, 1)

            rolled(dve, (0, 2, NG, NG), step, ch)

        @block.gpsimd
        def _(pool):
            ch = Chain(pool, pool_chain)
            link = ch.link
            GT = nc.gpsimd.tensor_tensor
            link(nc.gpsimd.memset(e_base[:], math.e))
            pool.wait_ge(par_loaded, 64)
            GT(dt[:], e_base[:], ldt[:], ALU.pow).then_inc(exp_ready, 1)
            link(nc.gpsimd.memset(ident[:], 0.0))
            nc.gpsimd.affine_select(out=ident[:], in_=ident[:], compare_op=ALU.not_equal, fill=1.0, base=0,
                                    pattern=[[-1, P]], channel_multiplier=1).then_inc(ident_ready, 1)
            nc.gpsimd.memset(g_blk[:], 0.0).then_inc(const_ready, 1)
            pt = sb("pt", [P, 2, GP - SPLIT, LB // 2])
            pu = sb("pu", [P, 2, GP - SPLIT, LB // 2])
            pool.wait_ge(tr_copied, CP_B + 3 * (KP // 2))

            def step(g, b, i):
                js = bass.ts(g, GP)
                if not (isinstance(g, int) and g < 2):
                    pool.wait_ge(blk_ready, 4 * g - 4)
                shape = [P, 2, C, GP]
                br = b_re[:, js].unsqueeze(1).unsqueeze(1).to_broadcast(shape)
                bi = b_im[:, :, js].unsqueeze(2).to_broadcast(shape)
                zr = z_re[:, KP - 1, js].unsqueeze(1).unsqueeze(1).to_broadcast(shape)
                zi = z_im[:, KP - 1, :, js].unsqueeze(2).to_broadcast(shape)
                for a, (src, fr, fi) in enumerate(((c_t[:, :, :, js], br, bi), (g_cmp[:, b, 0], zr, zi))):
                    link(GT(g_t[:], src, fr, ALU.mult))
                    link(GT(g_u[:], src, fi, ALU.mult))
                    last = GT(g_cmp[:, b, a], g_t[:], g_u[:, ::-1], ALU.add)
                    link(last)
                    pool.nop().then_inc(g_ready, 1)
                pool.wait_ge(w_low, g + 1)
                k, m, n = KP - 2, LB // 2, GP - SPLIT
                w = w_pow[:, b]
                jn = bass.ds(g * GP + SPLIT, n)
                zr = z_re[:, k, jn].unsqueeze(1).unsqueeze(3).to_broadcast([P, 2, n, m])
                zi = z_im[:, k, :, jn].unsqueeze(3).to_broadcast([P, 2, n, m])
                link(GT(pt[:], w[:, :, SPLIT:GP, 0:m], zr, ALU.mult))
                link(GT(pu[:], w[:, :, SPLIT:GP, 0:m], zi, ALU.mult))
                link(GT(w[:, :, SPLIT:GP, m:2 * m], pt[:], pu[:, ::-1], ALU.add))
                pool.nop().then_inc(w_pool, 1)

            rolled(pool, (0, 2, NG, NG), step, ch)

        @block.tensor
        def _(pe):
            pe.wait_ge(ident_ready, 1)
            pe.wait_ge(x_loaded, 64)
            for n in range(NCB):
                if n >= 4:
                    pe.wait_ge(tr_copied, n - 3)
                for c in range(2):
                    for r in range(2):
                        q = 2 * c + r
                        src = x_rows[:, 2 * n + c].rearrange("j (m r) -> j r m", r=2)[:, r]
                        last = nc.tensor.transpose(psum[n % 4][:, q * J:(q + 1) * J], src, ident[:])
                last.then_inc(tr_ready, 1)
            pe.wait_ge(par_loaded, 64)
            pe.wait_ge(tr_copied, NCB - 3)
            for r in range(2):
                src = b_rows[:].rearrange("j (m r) -> j r m", r=2)[:, r]
                last = nc.tensor.transpose(psum[NCB % 4][:, r * J:(r + 1) * J], src, ident[:])
            last.then_inc(tr_ready, 1)
            for q in range(KP // 2):
                pe.wait_ge(z_ready, q + 1)
                pe.wait_ge(tr_copied, NCB - 2 + q if q < 3 else CP_B)
                for k in range(2):
                    for r in range(2):
                        i = 2 * k + r
                        last = nc.tensor.transpose(psum[(NCB + 1 + q) % 4][:, i * J:(i + 1) * J],
                                                   z_rows[:, 2 * q + k, r], ident[:])
                last.then_inc(tr_ready, 1)
            pe.wait_ge(tr_copied, CP_B + 3 * (KP // 2))
            pe.wait_ge(const_ready, 3)

            def step(g, b, i):
                pe.wait_ge(blk_ready, 4 * g + 4)
                pe.wait_ge(w_dve, g + 1)
                pe.wait_ge(w_pool, g + 1)
                if not (isinstance(g, int) and g < 2):
                    pe.wait_ge(out_ready, 2 * g - 2)
                for q in range(QG):
                    bank, col = psum[2 * b + q // 4], (q % 4) * LB
                    for r in range(2):
                        for j in range(2):
                            last = nc.tensor.matmul(bank[64 * j:64 * j + 64, col:col + LB],
                                                    g_blk[:, b, r, 2 * q + j].rearrange("p s a c -> p (s a c)"),
                                                    w_pow[:, b, r, 2 * q + j], start=(r == 0), stop=(r == 1),
                                                    tile_position=(0, 64 * j))
                last.then_inc(prod_ready, 1)

            rolled(pe, (0, 2, NG, NG), step)


def attend(nc, h_dram, W_qkv, b_qkv, W_out, b_out, ident, psum, h_tok, y_t, y_dram):
    C, S, D = h_dram.shape
    NH, DH = 16, 16
    SCALE = 1.0 / DH ** 0.5
    QT = S // P
    DT = D // P
    H8 = NH // 2
    ZERO, MROW, KROWS = 64, 96, 98
    EPS = 1e-5
    GH = 4
    PBUF = 8
    S2B, POB, X, Y, SA, SB = 0, 2, 4, 5, 6, 7
    TT, TS, STT = nc.vector.tensor_tensor, nc.vector.tensor_scalar, nc.vector.scalar_tensor_tensor
    mm = nc.tensor.matmul
    SPAN = (-2, 2, C - 4, C + 2)

    with ExitStack() as ctx:
        def sb(name, shape, dt=F32):
            return ctx.enter_context(nc.sbuf_tensor(name, shape, dt))

        def sem(name):
            return ctx.enter_context(nc.semaphore(name))

        def sems(name, n):
            return [sem(f"{name}{i}") for i in range(n)]

        pr = sb("pr", [P, PBUF, QT, S])
        spare = pr[:].rearrange("p b t s -> p (b t s)")
        w_raw = spare[:, 0:6 * D].rearrange("p (t n) -> p t n", t=DT)
        wo_raw = spare[:, 6 * D:8 * D].rearrange("p (t n) -> p t n", t=DT)
        bo_rows = spare[:, 10 * D:11 * D]
        bv_cols = spare[:, 8 * D:8 * D + DT * P].rearrange("p (t n) -> p t n", t=DT)
        wqk = sb("wqk", [P, 2, DT, 4, DH, H8], F32R)
        wv = sb("wv", [P, 2, DT, D], F32R)
        wo = sb("wo", [P, 2, DT, D], F32R)
        bqk = sb("bqk", [P, 4])
        bv = sb("bv", [P, DT])
        bias_rows = sb("bias_rows", [P, D])
        xn = sb("xn", [P, QT, D])
        xt = sb("xt", [P, 2, 2, DT, S], F32R)
        qk = sb("qk", [P, 2, 2, 2, 2, S], F32R)
        qs = sb("qs", [P, 2, NH, S], F32R)
        ks = sb("ks", [P, 2, NH, S], F32R)
        mx = sb("mx", [P, QT, NH])
        mp = sb("mp", [H8, 2, S], F32R)
        va = sb("va", [P, 2, QT, NH, 32])
        o_sb = sb("o_sb", [P, 4, S])
        den = sb("den", [P, NH])
        on = xn
        ot = sb("ot", [P, 2, DT, S], F32R)
        y = o_sb[:, QT:2 * QT]
        bn = sb("bn", [P, 2, QT, 6])
        mv = sb("mv", [P, 2, QT, 2])
        vare = sb("vare", [P, 2, QT])
        rstd = sb("rstd", [P, 2, QT])
        half = sb("half", [P, QT])
        eps = sb("eps", [P, QT])

        w_loaded = sem("w_loaded")
        h_loaded = sems("h_loaded", 4)
        const2 = sem("const2")
        pool_const = sem("pool_const")
        bvb_ready = sem("bvb_ready")
        bias_ps = sem("bias_ps")
        bias_ready = sem("bias_ready")
        dve_chain, pool_chain = sem("dve_chain2"), sem("pool_chain2")
        ln1_stat, rstd1, xn_ready, hb = sem("ln1_stat"), sem("rstd1"), sem("xn_ready"), sem("hb")
        xt_ps, xt_hi, xt_lo = sem("xt_ps"), sem("xt_hi"), sem("xt_lo")
        q_ps, q_hi, q_lo = sem("q_ps"), sem("q_hi"), sem("q_lo")
        k_ps, k_hi, k_lo = sem("k_ps"), sem("k_hi"), sem("k_lo")
        v_ps, v_ready = sem("v_ps"), sem("v_ready")
        stk = [sems(f"stk{b}", 2) for b in range(2)]
        mrow = [sems(f"mrow{b}", 2) for b in range(2)]
        s1_ps, s1_max = sem("s1_ps"), sem("s1_max")
        mt_ps, m_hi, m_lo = sem("mt_ps"), sem("m_hi"), sem("m_lo")
        s2_ps, p_ready, pv_done, o_ready = sem("s2_ps"), sem("p_ready"), sem("pv_done"), sem("o_ready")
        ot_ps, on_ready = sem("ot_ps"), sem("on_ready")
        ont_ps, ont_hi, ont_lo = sem("ont_ps"), sem("ont_hi"), sem("ont_lo")
        pj_ps, h1_ready, ln2_stat, rstd2, y_ready = (sem("pj_ps"), sem("h1_ready"), sem("ln2_stat"), sem("rstd2"),
                                                     sem("y_ready"))
        r_done, yt_ps, yt_ready = sem("r_done"), sem("yt_ps"), sem("yt_ready")
        y_stored = sem("y_stored")

        def has(c):
            if not isinstance(c, int):
                return (True,) * 6
            return c + 3 < C, c + 2 < C, 0 <= c + 1 < C, 0 <= c < C, 0 <= c - 1 < C, 0 <= c - 2 < C

        def later(c, n):
            return not isinstance(c, int) or c >= n

        def first(eng, *counts):
            counts = [n if isinstance(n, int) or n is None else eng.compute_val(n) for n in counts]
            eng.wait_ge(w_loaded, 128)
            return counts

        def toks(c):
            return bass.ts(c, S)

        def tiles(c):
            return bass.ts(c, QT)

        block = ctx.enter_context(nc.Block())

        @block.sync
        def _(sp):
            def wl(dst, src, slow=False):
                sp.dma_start(dst, src, allow_slow_non_contiguous=slow).then_inc(w_loaded, 16)

            h_v = h_dram.rearrange("c (t p) d -> p (c t) d", p=P)
            n = C * QT // 4
            sp.dma_start(h_tok[:, 0:n], h_v[:, 0:n]).then_inc(h_loaded[0], 16)
            wl(w_raw, W_qkv.rearrange("(t p) n -> p t n", p=P))
            wl(wo_raw, W_out.rearrange("(t p) n -> p t n", p=P))
            for x in range(4):
                wl(bqk[:, x:x + 1], b_qkv[x * P:(x + 1) * P].rearrange("(h r) -> r h", r=DH), slow=True)
            wl(bv[:], b_qkv[2 * D:3 * D].rearrange("(t p) -> p t", p=P), slow=True)
            wl(bo_rows, b_out.partition_broadcast(P))
            for k in range(1, 4):
                sp.dma_start(h_tok[:, n * k:n * (k + 1)], h_v[:, n * k:n * (k + 1)]).then_inc(h_loaded[k], 16)

            def stack(a, b, s, used):
                made, used = first(sp, 2 * a + 2, used)
                for done in (q_hi, q_lo, k_hi, k_lo):
                    sp.wait_ge(done, made)
                if used is not None:
                    sp.wait_ge(s2_ps, used)
                for t, which, parts in ((qs, 0, (0, 0, 1, 1)), (ks, 1, (0, 1, 0, 1))):
                    for slot, part in enumerate(parts):
                        sp.dma_start(t[16 * slot:16 * slot + 16, b, H8 * s:H8 * s + H8].bitcast(F32),
                                     qk[:, b, which, part, s].bitcast(F32)).then_inc(stk[b][s], 16)

            def max_rows(n, b, s):
                made, used = first(sp, 2 * n + s + 1, 16 * n - 16 if later(n, 2) else None)
                sp.wait_ge(m_hi, made)
                sp.wait_ge(m_lo, made)
                if used is not None:
                    sp.wait_ge(s2_ps, used)
                for part in range(2):
                    sp.dma_start(qs[MROW + part:MROW + part + 1, b, H8 * s:H8 * s + H8].bitcast(F32),
                                 mp[:, part].bitcast(F32)).then_inc(mrow[b][s], 16)

            def step(c, b, i):
                ln, A, B, Cc, end, fin = has(c)
                if B:
                    stack(c + 1, 1 - b, 1, 16 * c if later(c, 1) else None)
                if Cc:
                    max_rows(c, b, 1)
                if A:
                    stack(c + 2, b, 0, 16 * c + 8 if later(c, 0) else None)
                if fin:
                    u = c - 2
                    made, = first(sp, QT * u + QT)
                    sp.wait_ge(y_ready, made)
                    sp.dma_start(y_dram[toks(u), :].rearrange("(t p) d -> p t d", p=P),
                                 y).then_inc(y_stored, 16)
                if B:
                    max_rows(c + 1, 1 - b, 0)

            rolled(sp, SPAN, step)
            sp.wait_ge(y_stored, 16 * C)

        @block.gpsimd
        def _(pool):
            ch = Chain(pool, pool_chain)
            link = ch.link
            GT = nc.gpsimd.tensor_tensor
            for n, (at, value) in enumerate(((half[:], -0.5), (va[:], 0.0), (va[:, :, :, :, DH:DH + 1], 1.0),
                                             (qs[ZERO:MROW].bitcast(F32), 0.0), (ks[ZERO:MROW].bitcast(F32), 0.0),
                                             (ks[MROW:KROWS].bitcast(F32), 1.0), (eps[:], EPS))):
                if n:
                    pool.wait_ge(pool_const, n)
                nc.gpsimd.memset(at, value).then_inc(pool_const, 1)
            pool.wait_ge(pool_const, 7)

            def power(which, stat, out, n):
                pool.wait_ge(stat, n)
                link(GT(vare[:, which], mv[:, which, :, 1], eps[:], ALU.add))
                GT(rstd[:, which], vare[:, which], half[:], ALU.pow).then_inc(out, 1)

            def add_bias(c):
                pool.wait_ge(xn_ready, QT * c + QT)
                ht = h_tok[:, tiles(c)]
                GT(ht, ht, bias_rows[:].unsqueeze(1).to_broadcast([P, QT, D]), ALU.add).then_inc(hb, 1)

            power(0, ln1_stat, rstd1, 1)
            pool.wait_ge(bias_ready, 1)
            add_bias(0)

            def step(c, b, i):
                ln, A, B, Cc, end, fin = has(c)
                if ln:
                    power(0, ln1_stat, rstd1, c + 4)
                    add_bias(c + 3)
                if fin:
                    u = c - 2
                    pool.wait_ge(y_ready, QT * u + QT)
                    GT(h_tok[:, tiles(u)], h_tok[:, tiles(u)], y, ALU.add).then_inc(r_done, 1)
                if end:
                    power(1, ln2_stat, rstd2, c)

            rolled(pool, SPAN, step, ch)

        @block.scalar
        def _(act):
            A_ = nc.scalar.activation
            act.wait_ge(w_loaded, 128)
            for dt in range(DT):
                A_(wqk[:, 0, dt].rearrange("p x r h -> p x h r"),
                   w_raw[:, dt, 0:2 * D].rearrange("p (x h r) -> p x h r", x=4, h=H8), ACT.Copy).then_inc(const2, 1)
            A_(wv[:, 0], w_raw[:, :, 2 * D:3 * D], ACT.Copy).then_inc(const2, 1)
            A_(wo[:, 0], wo_raw, ACT.Copy).then_inc(const2, 1)

            def step(c, b, i):
                ln, A, B, Cc, end, fin = has(c)
                a, d, t, u = c + 2, c + 1, c - 1, c - 2

                def max_hi(n, s):
                    act.wait_ge(mt_ps, 2 * n + s + 1)
                    if s or Cc:
                        act.wait_ge(mrow[b][1 - s], 32 * (i + 1))
                    A_(mp[:, 0], psum[(Y, X)[s]][0:H8, 0:S], ACT.Copy, scale=-1.0).then_inc(m_hi, 1)

                def parts_hi(which, bank, ps, hi):
                    act.wait_ge(ps, a + 1)
                    for s in range(2):
                        A_(qk[:, b, which, 0, s], psum[bank][:, s * S:(s + 1) * S], ACT.Identity,
                           bias=bqk[:, 2 * which + s:2 * which + s + 1]).then_inc(hi, 1)

                def o_copy(n, k):
                    act.wait_ge(pv_done, 4 * n + 2 * k + 2)
                    if later(n, 1):
                        act.wait_ge(ot_ps, 2 * n)
                    A_(o_sb[:, 2 * k:2 * k + 2].rearrange("p g s -> p (g s)"), psum[POB + k][:],
                       ACT.Copy).then_inc(o_ready, 1)

                for h in range(NH):
                    if h == 1 and A:
                        act.wait_ge(xt_ps, a + 1)
                        A_(xt[:, b, 0].rearrange("p t s -> p (t s)"), psum[Y][:], ACT.Copy).then_inc(xt_hi, 1)
                    if h == 2 and Cc:
                        max_hi(c, 1)
                    if h == 3 and end:
                        if later(u, 1):
                            act.wait_ge(y_stored, 16 * u)
                            act.wait_ge(r_done, u)
                            act.wait_ge(yt_ps, u)
                        o_copy(t, 1)
                    if h == 4 and A:
                        if later(c, 0):
                            act.wait_ge(stk[b][0], 128 * (i + 1))
                            act.wait_ge(stk[b][1], 128 * (i + 1))
                        parts_hi(0, X, q_ps, q_hi)
                    if h == 5 and A:
                        parts_hi(1, Y, k_ps, k_hi)
                    if h == 13 and fin:
                        act.wait_ge(yt_ps, u + 1)
                        A_(y_t[:, :, toks(u)], psum[X][:].rearrange("p (t s) -> p t s", t=DT),
                           ACT.Copy).then_inc(yt_ready, 1)
                    if h == 10 and B:
                        max_hi(d, 0)
                    if h == 11 and Cc:
                        o_copy(c, 0)
                    if h == 11 and end:
                        act.wait_ge(ont_ps, t + 1)
                        if later(t, 1):
                            act.wait_ge(pj_ps, t)
                        A_(ot[:, 0].rearrange("p t s -> p (t s)"), psum[X][:], ACT.Copy).then_inc(ont_hi, 1)
                    if Cc:
                        act.wait_ge(s2_ps, 16 * c + h + 1)
                        if h >= PBUF or later(c, 1):
                            act.wait_ge(pv_done, 4 * c + h // GH - 1)
                        A_(pr[:, h % PBUF].rearrange("p t s -> p (t s)"), psum[S2B + h % 2][:], ACT.Exp,
                           scale=SCALE).then_inc(p_ready, 1)
                if B:
                    act.wait_ge(v_ps, d + 1)
                    if later(c, 1):
                        act.wait_ge(pv_done, 4 * c)
                    else:
                        act.wait_ge(pool_const, 7)
                    A_(va[:, 1 - b, :, :, 0:DH], psum[X][:].rearrange("p (t h r) -> p t h r", t=QT, h=NH),
                       ACT.Copy).then_inc(v_ready, 1)

            rolled(act, SPAN, step)

        @block.vector
        def _(dve):
            ch = Chain(dve, dve_chain)
            link = ch.link

            def stats(which, tile):
                for t in range(QT):
                    ch.tick(nc.vector.bn_stats(bn[:, which, t], tile(t)))

            def written():
                dve.wait_ge(dve_chain, ch.base + ch.k)

            def collect(which, done):
                for t in range(QT):
                    last = nc.vector.bn_aggr(mv[:, which, t], bn[:, which, t])
                    if t < QT - 1:
                        ch.tick(last)
                last.then_inc(done, 1)

            def normal(which, out, src, done):
                for t in range(QT):
                    TS(out[:, t], src(t), mv[:, which, t, 0:1], rstd[:, which, t:t + 1], ALU.subtract,
                       ALU.mult).then_inc(done, 1)

            def ln1_stats(c):
                stats(0, lambda t: h_tok[:, c * QT + t])

            def ln1(c):
                dve.wait_ge(rstd1, c + 1)
                if later(c, 1):
                    dve.wait_ge(xt_ps, c)
                normal(0, xn, lambda t: h_tok[:, c * QT + t], xn_ready)

            dve.wait_ge(h_loaded[0], 16)
            ln1_stats(0)
            written()
            collect(0, ln1_stat)
            link(nc.vector.memset(bv_cols, 1.0))
            ln1(0)
            dve.wait_ge(w_loaded, 128)
            dve.wait_ge(const2, 4)
            for dt in range(DT):
                src = w_raw[:, dt, 0:2 * D].rearrange("p (x h r) -> p x h r", x=4, h=H8)
                TT(wqk[:, 1, dt].rearrange("p x r h -> p x h r"), src,
                   wqk[:, 0, dt].bitcast(F32).rearrange("p x r h -> p x h r"), ALU.subtract).then_inc(const2, 1)
            TT(wv[:, 1], w_raw[:, :, 2 * D:3 * D], wv[:, 0].bitcast(F32), ALU.subtract).then_inc(const2, 1)
            TT(wo[:, 1], wo_raw, wo[:, 0].bitcast(F32), ALU.subtract).then_inc(const2, 1)
            for dt in range(DT):
                TS(bv_cols[:, dt], bv_cols[:, dt], bv[:, dt:dt + 1], None, ALU.mult).then_inc(bvb_ready, 1)
            dve.wait_ge(bias_ps, 1)
            TT(bias_rows[:], psum[S2B][:, 0:D], bo_rows, ALU.add).then_inc(bias_ready, 1)

            def step(c, b, i):
                ln, A, B, Cc, end, fin = has(c)
                a, d, t, u = c + 2, c + 1, c - 1, c - 2

                def max_lo(n, s):
                    dve.wait_ge(m_hi, 2 * n + s + 1)
                    STT(out=mp[:, 1], in0=psum[(Y, X)[s]][0:H8, 0:S], scalar=-1.0,
                        in1=mp[:, 0].bitcast(F32), op0=ALU.mult, op1=ALU.subtract).then_inc(m_lo, 1)

                def parts_lo(which, bank, hi, lo):
                    dve.wait_ge(hi, 2 * a + 2)
                    for s in range(2):
                        STT(out=qk[:, b, which, 1, s], in0=psum[bank][:, s * S:(s + 1) * S],
                            scalar=bqk[:, 2 * which + s:2 * which + s + 1], in1=qk[:, b, which, 0, s].bitcast(F32),
                            op0=ALU.add, op1=ALU.subtract).then_inc(lo, 1)

                def normalize_o(q, bank):
                    dve.wait_ge(ot_ps, 2 * t + q + 1)
                    o_v = psum[bank][:].rearrange("p (h r) -> p h r", h=NH)
                    link(nc.vector.reciprocal(den[:], o_v[:, :, DH]))
                    TT(on[:, q].rearrange("p (h r) -> p h r", h=NH), o_v[:, :, 0:DH],
                       den[:].unsqueeze(2).to_broadcast([P, NH, DH]), ALU.mult).then_inc(on_ready, 1)

                for h in range(NH):
                    if h == 2 and A:
                        dve.wait_ge(xt_hi, a + 1)
                        TT(xt[:, b, 1].rearrange("p t s -> p (t s)"), psum[Y][:],
                           xt[:, b, 0].bitcast(F32).rearrange("p t s -> p (t s)"), ALU.subtract).then_inc(xt_lo, 1)
                    if h == 3 and Cc:
                        max_lo(c, 1)
                    if h == 5 and A:
                        parts_lo(0, X, q_hi, q_lo)
                    if h == 6 and A:
                        parts_lo(1, Y, k_hi, k_lo)
                    if h == 8 and end:
                        normalize_o(0, Y)
                    if h == 9 and end:
                        dve.wait_ge(on_ready, 2 * t + 1)
                        normalize_o(1, X)
                    if h == 9 and fin:
                        dve.wait_ge(rstd2, u + 1)
                        if later(u, 1):
                            dve.wait_ge(y_stored, 16 * u)
                            dve.wait_ge(yt_ps, u)
                            dve.wait_ge(r_done, u)
                        normal(1, y, lambda q: h_tok[:, u * QT + q], y_ready)
                    if h == 11 and B:
                        max_lo(d, 0)
                    if h == 12 and end:
                        dve.wait_ge(ont_hi, t + 1)
                        TT(ot[:, 1].rearrange("p t s -> p (t s)"), psum[X][:],
                           ot[:, 0].bitcast(F32).rearrange("p t s -> p (t s)"), ALU.subtract).then_inc(ont_lo, 1)
                    if h == 14 and end:
                        dve.wait_ge(pj_ps, t + 1)
                        dve.wait_ge(hb, t + 1)
                        ht = h_tok[:, tiles(t)]
                        TT(ht, psum[Y][:].rearrange("p (t d) -> p t d", t=QT), ht, ALU.add).then_inc(h1_ready, 1)
                        dve.wait_ge(h1_ready, t + 1)
                    if (h == 15 and end) or (h == 5 and ln):
                        written()
                    if B:
                        if h == 0 and later(d, 1):
                            dve.wait_ge(mt_ps, 2 * d - 1)
                        if h == H8 and later(c, 0):
                            dve.wait_ge(mt_ps, 2 * c + 2)
                        dve.wait_ge(s1_ps, 16 * d + h + 1)
                        nc.vector.tensor_reduce(mx[:, :, h], psum[SA + h % 2][:].rearrange("p (t s) -> p t s", t=QT),
                                                AX.X, ALU.max).then_inc(s1_max, 1)
                    if h == 4 and ln:
                        if isinstance(c, int):
                            for k in range(4):
                                if k == (c + 3) // 4 or c == 1:
                                    dve.wait_ge(h_loaded[k], 16)
                        ln1_stats(c + 3)
                    if h == 5 and ln:
                        collect(0, ln1_stat)
                    if h == 13 and ln:
                        ln1(c + 3)
                    if h == 14 and end:
                        stats(1, lambda q: h_tok[:, t * QT + q])
                    if h == 15 and end:
                        collect(1, ln2_stat)

            rolled(dve, SPAN, step, ch)

        @block.tensor
        def _(pe):
            def product(out, pairs):
                for k, (l, r) in enumerate(pairs):
                    last = mm(out, l, r, start=(k == 0), stop=(k == len(pairs) - 1))
                return last

            PARTS = ((0, 0), (1, 0), (0, 1))
            pe.wait_ge(bvb_ready, DT)
            for dt in range(DT):
                last = mm(psum[S2B][:, 0:D], bv_cols[:, dt], wo_raw[:, dt], start=(dt == 0), stop=(dt == DT - 1))
            last.then_inc(bias_ps, 1)
            pe.wait_ge(const2, 8)
            pe.wait_ge(pool_const, 7)
            pe.wait_ge(bias_ready, 1)

            def step(c, b, i):
                ln, A, B, Cc, end, fin = has(c)
                a, d, t, u = c + 2, c + 1, c - 1, c - 2

                def free(n, *read):
                    for done in read:
                        pe.wait_ge(done, n)

                def four(bank, src):
                    for dt in range(DT):
                        for q in range(QT):
                            last = nc.tensor.transpose(psum[bank][:, dt * S + q * P:dt * S + (q + 1) * P],
                                                       src[:, q, dt * P:(dt + 1) * P], ident[:])
                    return last

                def x_transposed():
                    pe.wait_ge(xn_ready, QT * a + QT)
                    if later(t, 1):
                        free(t, h1_ready)
                    elif later(d, 1):
                        free(2 * d - 1, m_hi, m_lo)
                    elif later(a, 1):
                        free(2 * a, k_hi, k_lo)
                    four(Y, xn).then_inc(xt_ps, 1)

                def max_transposed(n, s):
                    pe.wait_ge(s1_max, 16 * n + 8 * s + 8)
                    if s:
                        free(n + 1, v_ready)
                    elif end:
                        free(2 * t + 1, on_ready)
                    else:
                        free(2 * a + 2, k_hi, k_lo)
                    for q in range(QT):
                        last = nc.tensor.transpose(psum[(Y, X)[s]][0:H8, q * P:(q + 1) * P],
                                                   mx[:, q, H8 * s:H8 * s + H8], ident[:])
                    last.then_inc(mt_ps, 1)

                def q_or_k(which, bank, done):
                    for s in range(2):
                        last = product(psum[bank][:, s * S:(s + 1) * S],
                                       [(wqk[:, l, dt, 2 * which + s].rearrange("p r h -> p (r h)"), xt[:, b, r, dt])
                                        for dt in range(DT) for l, r in PARTS])
                    last.then_inc(done, 1)

                def q_product():
                    if Cc:
                        free(2 * c + 2, m_hi, m_lo)
                    elif later(a, 1):
                        free(2 * a, q_hi, q_lo)
                    pe.wait_ge(xt_hi, a + 1)
                    pe.wait_ge(xt_lo, a + 1)
                    q_or_k(0, X, q_ps)

                def y_transposed():
                    pe.wait_ge(y_ready, QT * u + QT)
                    if end:
                        free(t + 1, ont_hi, ont_lo)
                    else:
                        free(u, yt_ready)
                    four(X, y).then_inc(yt_ps, 1)

                def o_transposed(q):
                    if q:
                        if A:
                            free(2 * a + 2, q_hi, q_lo)
                        elif Cc:
                            free(2 * c + 2, m_hi, m_lo)
                        else:
                            free(u, yt_ready)
                    else:
                        pe.wait_ge(o_ready, 2 * t + 2)
                        if A:
                            free(2 * a + 2, k_hi, k_lo)
                        else:
                            free(t, h1_ready)
                    for g in range(4):
                        last = nc.tensor.transpose(psum[(Y, X)[q]][:, g * P:(g + 1) * P],
                                                   o_sb[:, g, q * P:(q + 1) * P], ident[:])
                    last.then_inc(ot_ps, 1)

                def projection():
                    if B:
                        free(2 * d + 1, m_hi, m_lo)
                    pe.wait_ge(ont_hi, t + 1)
                    pe.wait_ge(ont_lo, t + 1)
                    for q in range(QT):
                        last = product(psum[Y][:, q * D:(q + 1) * D],
                                       [(ot[:, l, dt, q * P:(q + 1) * P], wo[:, r, dt])
                                        for dt in range(DT) for l, r in PARTS])
                    last.then_inc(pj_ps, 1)

                def v_product():
                    if fin:
                        free(u + 1, yt_ready)
                    elif end:
                        free(t + 1, ont_hi, ont_lo)
                    else:
                        free(2 * a + 2, q_hi, q_lo)
                    for q in range(QT):
                        last = product(psum[X][:, q * D:(q + 1) * D],
                                       [(xt[:, 1 - b, l, dt, q * P:(q + 1) * P], wv[:, r, dt])
                                        for dt in range(DT) for l, r in PARTS])
                    last.then_inc(v_ps, 1)

                def pv(n, g, buf):
                    pe.wait_ge(p_ready, 16 * n + GH * g + GH)
                    if g == 0:
                        pe.wait_ge(v_ready, n + 1)
                    if g % 2 == 0 and later(n, 1):
                        pe.wait_ge(o_ready, 2 * n - 1 + g // 2)
                    for kt in range(QT):
                        for j in range(GH):
                            h = GH * g + j
                            last = mm(psum[POB + g // 2][32 * j:32 * j + 32, (g % 2) * S:(g % 2 + 1) * S],
                                      va[:, buf, kt, h], pr[:, h % PBUF, kt], start=(kt == 0), stop=(kt == QT - 1),
                                      tile_position=(0, 32 * j))
                    last.then_inc(pv_done, 1)

                for h in range(NH):
                    if B:
                        if h % H8 == 0:
                            pe.wait_ge(stk[1 - b][h // H8], 128 * (i + b + 1))
                        if h >= 2 or later(d, 1):
                            pe.wait_ge(s1_max, 16 * d + h - 1)
                        for q in range(QT):
                            last = mm(psum[SA + h % 2][:, q * S:(q + 1) * S], qs[0:MROW, 1 - b, h, q * P:(q + 1) * P],
                                      ks[0:MROW, 1 - b, h], start=True, stop=True)
                        last.then_inc(s1_ps, 1)
                    if Cc:
                        if h % H8 == 0:
                            pe.wait_ge(mrow[b][h // H8], 32 * (i + 1))
                        if h >= 2 or later(c, 1):
                            pe.wait_ge(p_ready, 16 * c + h - 1)
                        for kt in range(QT):
                            last = mm(psum[S2B + h % 2][:, kt * S:(kt + 1) * S], ks[0:KROWS, b, h, kt * P:(kt + 1) * P],
                                      qs[0:KROWS, b, h], start=True, stop=True)
                        last.then_inc(s2_ps, 1)
                        if h in (5, 9, 13):
                            pv(c, (h - 5) // 4, b)
                    if h == 0 and A:
                        x_transposed()
                    if h == 1 and end:
                        pv(t, 3, 1 - b)
                    if h == 1 and Cc:
                        max_transposed(c, 1)
                    if h == 3 and A:
                        q_product()
                    if h == 4 and A:
                        q_or_k(1, Y, k_ps)
                    if h == 6 and end:
                        o_transposed(0)
                    if h == 7 and end:
                        o_transposed(1)
                    if h == 9 and B:
                        max_transposed(d, 0)
                    if h == 10 and end:
                        pe.wait_ge(on_ready, 2 * t + 2)
                        four(X, on).then_inc(ont_ps, 1)
                    if h == 12 and fin:
                        y_transposed()
                    if h == 13 and end:
                        projection()
                    if h == 14 and B:
                        v_product()

            rolled(pe, SPAN, step)


def route(nc, router_w, router_b, ident, psum, y_t, slot_to, slot_of, gate, token_id, table_dram, CAP):
    D, E = router_w.shape
    DT = D // P
    T = y_t.shape[2] // P
    NCH = T // 4
    NSLOT = E * CAP
    LG, CUM, TOT = 4, 5, 6
    V = nc.vector
    TT, TS, STT, RED = V.tensor_tensor, V.tensor_scalar, V.scalar_tensor_tensor, V.tensor_reduce

    with ExitStack() as ctx:
        def sb(name, shape, dt=F32):
            return ctx.enter_context(nc.sbuf_tensor(name, shape, dt))

        def sem(name):
            return ctx.enter_context(nc.semaphore(name))

        rw = sb("rw", [P, DT, E])
        rb = sb("rb", [E, 1])
        lg_t = sb("lg_t", [E, T * P])
        em = sb("em", [P, T, E])
        em_i = sb("em_i", [P, T, E], I32)
        prob = sb("prob", [P, T, E])
        ex = sb("ex", [P, T, E])
        hot = sb("hot", [P, 2, T, E])
        both = sb("both", [P, T, E])
        work = sb("work", [P, T, E])
        rest = sb("rest", [P, T, E])
        pos = sb("pos", [P, T, E])
        tot = sb("tot", [P, E, T])
        run = sb("run", [P, E, T])
        keep = sb("keep", [P, E, T])
        best = sb("best", [P, 2, T])
        idx = sb("idx", [P, 2, T])
        place = sb("place", [P, 2, T])
        fits = sb("fits", [P, 2, T])
        s_a = sb("s_a", [P, T])
        s_b = sb("s_b", [P, T])
        slot_f = sb("slot_f", [P, 2, T])
        slot_g = sb("slot_g", [P, 2, T])
        before = sb("before", [P, P])
        ones = sb("ones", [P, P])
        zero = sb("zero", [P, NSLOT // P], U32)

        loaded, zeroed = sem("r_loaded"), sem("r_zeroed")
        const_r = sem("const_r")
        lt_ps, lt_ready, lg_ps = sem("lt_ps"), sem("lt_ready"), sem("lg_ps")
        shifted, exp_done = sem("shifted"), sem("exp_done")
        hot_ready, cum_ps, chain = sem("hot_ready"), sem("cum_ps"), sem("r_chain")

        block = ctx.enter_context(nc.Block())

        @block.sync
        def _(sp):
            sp.dma_start(rw[:], router_w.rearrange("(t p) e -> p t e", p=P)).then_inc(loaded, 16)
            sp.dma_start(rb[:], router_b.rearrange("(e o) -> e o", o=1)).then_inc(loaded, 16)
            sp.wait_ge(const_r, 7)
            sp.dma_start(table_dram.rearrange("(p s) o -> p (s o)", p=P), zero[:]).then_inc(zeroed, 16)
            sp.wait_ge(zeroed, 16)

        @block.gpsimd
        def _(pool):
            G = nc.gpsimd
            G.memset(ones[:], 1.0).then_inc(const_r, 1)
            pool.wait_ge(const_r, 1)
            G.affine_select(out=before[:], in_=ones[:], compare_op=ALU.is_ge, fill=0.0, base=-1,
                            pattern=[[1, P]], channel_multiplier=-1).then_inc(const_r, 1)
            G.iota(em_i[:], pattern=[[0, T], [1, E]], base=-E, channel_multiplier=0).then_inc(const_r, 1)
            G.iota(token_id[:], pattern=[[P, T]], base=0, channel_multiplier=1).then_inc(const_r, 1)
            G.memset(keep[:], 1.0).then_inc(const_r, 1)
            pool.wait_ge(const_r, 5)
            G.memset(keep[:, :, 0:1], 0.0).then_inc(const_r, 1)
            G.memset(zero[:], 0).then_inc(const_r, 1)

        @block.scalar
        def _(act):
            act.wait_ge(loaded, 32)
            for n in range(NCH):
                act.wait_ge(lt_ps, n + 1)
                nc.scalar.activation(lg_t[:, n * 512:(n + 1) * 512], psum[n % 4][0:E, :], ACT.Identity,
                                     bias=rb[:, 0:1]).then_inc(lt_ready, 1)
            act.wait_ge(shifted, 1)
            nc.scalar.activation(ex[:], work[:], ACT.Exp).then_inc(exp_done, 1)

        @block.tensor
        def _(pe):
            pe.wait_ge(loaded, 32)
            for n in range(NCH):
                if n >= 4:
                    pe.wait_ge(lt_ready, n - 3)
                for dt in range(DT):
                    last = nc.tensor.matmul(psum[n % 4][0:E, :], rw[:, dt], y_t[:, dt, n * 512:(n + 1) * 512],
                                            start=(dt == 0), stop=(dt == DT - 1))
                last.then_inc(lt_ps, 1)
            for n in range(NCH):
                pe.wait_ge(lt_ready, n + 1)
                for k in range(4):
                    t = 4 * n + k
                    last = nc.tensor.transpose(psum[LG][:, t * E:(t + 1) * E], lg_t[:, t * P:(t + 1) * P],
                                               ident[0:E, 0:E])
            last.then_inc(lg_ps, 1)
            pe.wait_ge(hot_ready, 1)
            pe.wait_ge(const_r, 2)
            flat = both[:].rearrange("p t e -> p (t e)")
            nc.tensor.matmul(psum[CUM][:], before[:], flat, start=True, stop=True)
            nc.tensor.matmul(psum[TOT][:], ones[:], flat, start=True, stop=True).then_inc(cum_ps, 1)

        @block.vector
        def _(dve):
            link = Chain(dve, chain).link
            per_tile = lambda x: x.unsqueeze(2).to_broadcast([P, T, E])
            te = lambda b: psum[b][:].rearrange("p (t e) -> p t e", t=T)
            dve.wait_ge(const_r, 7)
            link(V.tensor_copy(em[:], em_i[:]))
            dve.wait_ge(lg_ps, 1)
            link(RED(s_a[:], te(LG), AX.X, ALU.max))
            TT(work[:], te(LG), per_tile(s_a[:]), ALU.subtract).then_inc(shifted, 1)
            dve.wait_ge(exp_done, 1)
            link(RED(s_b[:], ex[:], AX.X, ALU.add))
            link(V.reciprocal(s_a[:], s_b[:]))
            link(TT(prob[:], ex[:], per_tile(s_a[:]), ALU.mult))
            for k, src in ((0, prob), (1, rest)):
                link(RED(best[:, k], src[:], AX.X, ALU.max))
                link(TT(work[:], src[:], per_tile(best[:, k]), ALU.is_equal))
                link(TT(work[:], work[:], em[:], ALU.mult))
                link(RED(idx[:, k], work[:], AX.X, ALU.min))
                link(TT(hot[:, k], em[:], per_tile(idx[:, k]), ALU.is_equal))
                if k == 0:
                    link(STT(out=rest[:], in0=hot[:, 0], scalar=-4.0, in1=prob[:], op0=ALU.mult, op1=ALU.add))
            TT(both[:], hot[:, 0], hot[:, 1], ALU.add).then_inc(hot_ready, 1)
            link(TT(s_a[:], best[:, 0], best[:, 1], ALU.add))
            link(TS(s_a[:], s_a[:], 1e-9, None, ALU.add))
            link(V.reciprocal(s_b[:], s_a[:]))
            dve.wait_ge(cum_ps, 1)
            link(V.tensor_copy(tot[:], psum[TOT][:].rearrange("p (t e) -> p e t", t=T)))
            link(V.tensor_tensor_scan(run[:].rearrange("p e t -> p (e t)"), keep[:].rearrange("p e t -> p (e t)"),
                                      tot[:].rearrange("p e t -> p (e t)"), 0.0, ALU.mult, ALU.add))
            link(TT(run[:], run[:], tot[:], ALU.subtract))
            link(TT(pos[:], te(CUM), run[:].rearrange("p e t -> p t e"), ALU.add))
            for k in range(2):
                link(TT(work[:], hot[:, k], pos[:], ALU.mult))
                link(RED(place[:, k], work[:], AX.X, ALU.add))
            link(TS(fits[:], place[:], float(CAP), None, ALU.is_lt))
            link(TS(slot_g[:], place[:], float(CAP - 1), float(E * CAP), ALU.min, ALU.add))
            link(STT(out=slot_f[:], in0=idx[:], scalar=float(CAP), in1=slot_g[:], op0=ALU.mult, op1=ALU.add))
            link(TS(place[:], fits[:], float(-2 * NSLOT), float(2 * NSLOT), ALU.mult, ALU.add))
            link(TT(slot_g[:], slot_f[:], place[:], ALU.add))
            link(V.tensor_copy(slot_of[:], slot_f[:]))
            link(V.tensor_copy(slot_to[:], slot_g[:]))
            link(TT(gate[:], best[:], fits[:], ALU.mult))
            link(TT(gate[:], gate[:], s_b[:].unsqueeze(1).to_broadcast([P, 2, T]), ALU.mult))


def experts(nc, W, ident, psum, h_tok, y_t, y_dram, slot_to, slot_of, gate, token_id, table_dram, e_dram,
            out, CAP):
    w_gate, w_up, w_down, sw_gate, sw_up, sw_down = W
    E, D, F = w_gate.shape
    DT = D // P
    FT = -(-F // P)
    FW = [min(P, F - P * f) for f in range(FT)]
    T = y_t.shape[2] // P
    NS = CAP // P
    NSLOT = E * CAP
    XB0, GB, UB, DB = 0, 2, 4, 6
    V, A_, G = nc.vector, nc.scalar.activation, nc.gpsimd
    TT, STT = V.tensor_tensor, V.scalar_tensor_tensor
    mm = nc.tensor.matmul
    PARTS = ((0, 0), (1, 0), (0, 1))
    HALF = T // 8
    YG = 8

    with ExitStack() as ctx:
        def sb(name, shape, dt=F32):
            return ctx.enter_context(nc.sbuf_tensor(name, shape, dt))

        sgu = sb("sgu", [P, 2, DT, 2, F], F32R)
        sdn = sb("sdn", [P, 2, FT, D], F32R)
        egu = sb("egu", [P, 2, 2, DT, 2, F], F32R)
        edn = sb("edn", [P, 2, 2, FT, D], F32R)
        raw = sb("raw", [P, 2, DT * 2 * F + FT * D])
        xt = sb("xt4", [P, 2, 2, DT * CAP], F32R)
        hid = sb("hid", [P, 2, 2, FT, CAP], F32R)
        sg = sb("sg", [P, 2, 512])
        hf = sb("hf", [P, 2, 512])
        xg = sb("xg", [P, 2, NS, D])
        yb = sb("yb", [P, NS, D])
        slots = sb("slots", [P, E, NS], U32)
        yg = raw[:].rearrange("p b n -> p (b n)")[:, 0:YG * 2 * D].rearrange("p (k m d) -> p k m d", k=YG, m=2)
        NGU = DT * 2 * F

        def raw_views(b):
            return (raw[:, b, 0:NGU].rearrange("p (t g f) -> p t g f", t=DT, g=2),
                    raw[:, b, NGU:].rearrange("p (t d) -> p t d", t=FT))

        def load_weights(sp, b, wg, wu, wd, done):
            gu, dn = raw_views(b)
            for k, w in ((0, wg), (1, wu)):
                sp.dma_start(gu[:, :, k], w.rearrange("(t p) f -> p t f", p=P)).then_inc(done, 16)
            sp.dma_start(dn[:, 0:FT - 1], wd[0:(FT - 1) * P].rearrange("(t p) d -> p t d", p=P)).then_inc(done, 16)
            sp.dma_start(dn[0:FW[-1], FT - 1], wd[(FT - 1) * P:F]).then_inc(done, 16)

        def split_pieces(b, gu, dn):
            rgu, rdn = raw_views(b)
            r = FW[-1]
            return [(rgu, gu[:, 0], gu[:, 1]), (rdn[:, 0:FT - 1], dn[:, 0, 0:FT - 1], dn[:, 1, 0:FT - 1]),
                    (rdn[0:r, FT - 1], dn[0:r, 0, FT - 1], dn[0:r, 1, FT - 1])]

        def phase(name, shared, n_units, span, first_tile, more_sems, sp_more, pool_more, dve_more,
                  weights_in=False):
            with ExitStack() as pctx:
                def sem(s):
                    return pctx.enter_context(nc.semaphore(f"{s}_{name}"))

                NT = 4 if shared else NS
                N = NT * P
                COLS = [(0, N)] if shared else [(0, N // 2), (N // 2, N // 2)]
                K = FT * len(COLS)
                R = (NT + 1) // 2
                XB = -(-DT * NS * P // 512)
                x_ps, x_hi, x_lo = sem("x_ps"), sem("x_hi"), sem("x_lo")
                gu_ps, sg_ready, hf_ready = sem("gu_ps"), sem("sg_ready"), sem("hf_ready")
                hh_ready, hl_ready = sem("hh_ready"), sem("hl_ready")
                d_ps, d_done = sem("d_ps"), sem("d_done")
                w_hi, w_lo = sem("w_hi"), sem("w_lo")
                w_in = [sem("w_in0"), sem("w_in1")] if not shared or weights_in else None
                g_in, y_out = (None, None) if shared else ([sem("g_in0"), sem("g_in1")],
                                                           [sem("y_out0"), sem("y_out1")])
                extra = {k: sem(k) for k in more_sems}
                NX = 1 if shared else XB

                def later(n, k):
                    return not isinstance(n, int) or n >= k

                def gu_w(b, part, dt, k, f):
                    w = sgu[:, part] if shared else egu[:, b, part]
                    return w[:, dt, k, f * P:f * P + FW[f]]

                def dn_w(b, part, f):
                    w = sdn[:, part] if shared else edn[:, b, part]
                    return w[0:FW[f], f]

                def x_view(b, part):
                    return xt[:, b, part, 0:DT * N].rearrange("p (t s) -> p t s", t=DT)

                block = pctx.enter_context(nc.Block())

                @block.tensor
                def _(pe):
                    def gate_up(n, b):
                        if shared:
                            if isinstance(n, int) and n == 0:
                                pe.wait_ge(w_lo, 3)
                                pe.wait_ge(w_hi, 3)
                        else:
                            pe.wait_ge(w_lo, 3 * n + 3)
                            pe.wait_ge(w_hi, 3 * n + 3)
                        pe.wait_ge(x_hi, NX * n + NX)
                        pe.wait_ge(x_lo, NX * n + NX)
                        for c, (c0, cw) in enumerate(COLS):
                            for f in range(FT):
                                j = c * FT + f
                                q = K * n + j
                                k = (K * b + j) % 2
                                if later(n, 1) or j >= 2:
                                    pe.wait_ge(hf_ready, q - 1)
                                for g, bank in ((0, GB), (1, UB)):
                                    m = 0
                                    for dt in range(DT):
                                        for l, r in PARTS:
                                            last = mm(psum[bank + k][0:FW[f], 0:cw], gu_w(b, l, dt, g, f),
                                                      x_view(b, r)[:, dt, c0:c0 + cw], start=(m == 0),
                                                      stop=(m == 3 * DT - 1))
                                            m += 1
                                last.then_inc(gu_ps, 1)

                    def turn(n, b):
                        if shared:
                            return
                        pe.wait_ge(g_in[b], 80 * (n // 2 + 1) if isinstance(n, int) else 80 * self_i[0] + 80)
                        for j in range(XB):
                            k = (XB * b + j) % 2
                            if later(n, 1) or j >= 2:
                                pe.wait_ge(x_lo, XB * n + j - 1)
                            for m in range(4 * j, min(4 * j + 4, DT * NS)):
                                dt, s = divmod(m, NS)
                                last = nc.tensor.transpose(psum[XB0 + k][:, (m % 4) * P:(m % 4 + 1) * P],
                                                           xg[:, b, s, dt * P:(dt + 1) * P], ident[:])
                            last.then_inc(x_ps, 1)

                    def down(n, b):
                        pe.wait_ge(hh_ready, K * n + K)
                        pe.wait_ge(hl_ready, K * n + K)
                        for j in range(R):
                            k = (R * b + j) % 2
                            if later(n, 1) or j >= 2:
                                pe.wait_ge(d_done, R * n + j - 1)
                            for s in range(2 * j, min(2 * j + 2, NT)):
                                m = 0
                                for f in range(FT):
                                    for l, r in PARTS:
                                        last = mm(psum[DB + k][:, (s % 2) * D:(s % 2 + 1) * D],
                                                  hid[0:FW[f], b, l, f, s * P:(s + 1) * P], dn_w(b, r, f),
                                                  start=(m == 0), stop=(m == 3 * FT - 1))
                                        m += 1
                            last.then_inc(d_ps, 1)

                    self_i = [0]
                    turn(0, 0)

                    def step(n, b, i):
                        gate_up(n, b)
                        if not isinstance(n, int) or n + 1 < n_units:
                            self_i[0] = i + b
                            turn(n + 1, 1 - b)
                        down(n, b)

                    rolled(pe, span, step)

                @block.scalar
                def _(act):
                    def take_x(n, b):
                        if later(n, 2):
                            act.wait_ge(gu_ps, K * n - K)
                        if shared:
                            t0 = (first_tile + NT * n) * P
                            A_(x_view(b, 0), y_t[:, :, t0:t0 + N], ACT.Copy).then_inc(x_hi, 1)
                        else:
                            for j in range(XB):
                                act.wait_ge(x_ps, XB * n + j + 1)
                                w = min(512, DT * N - 512 * j)
                                A_(xt[:, b, 0, 512 * j:512 * j + w], psum[XB0 + (XB * b + j) % 2][:, 0:w],
                                   ACT.Copy).then_inc(x_hi, 1)

                    def hi(n, b, j):
                        c0, cw = COLS[j // FT]
                        f = j % FT
                        k = (K * b + j) % 2
                        act.wait_ge(hf_ready, K * n + j + 1)
                        if j == 0 and later(n, 2):
                            act.wait_ge(d_ps, R * n - R)
                        A_(hid[0:FW[f], b, 0, f, c0:c0 + cw], hf[0:FW[f], k, 0:cw], ACT.Copy).then_inc(hh_ready, 1)

                    def step(n, b, i):
                        for j in range(K):
                            f = j % FT
                            cw = COLS[j // FT][1]
                            k = (K * b + j) % 2
                            act.wait_ge(gu_ps, K * n + j + 1)
                            if later(n, 1) or j >= 2:
                                act.wait_ge(hf_ready, K * n + j - 1)
                            A_(sg[0:FW[f], k, 0:cw], psum[GB + k][0:FW[f], 0:cw], ACT.Silu).then_inc(sg_ready, 1)
                            if j:
                                hi(n, b, j - 1)
                        hi(n, b, K - 1)
                        if not isinstance(n, int) or n + 1 < n_units:
                            take_x(n + 1, 1 - b)
                        if not shared:
                            for j in range(R):
                                act.wait_ge(d_ps, R * n + j + 1)
                                if j == 0 and later(n, 1):
                                    act.wait_ge(y_out[1 - b], 16 * (i + b))
                                w = min(2, NT - 2 * j)
                                A_(yb[:, 2 * j:2 * j + w].rearrange("p s d -> p (s d)"),
                                   psum[DB + (R * b + j) % 2][:, 0:w * D], ACT.Copy).then_inc(d_done, 1)

                    take_x(0, 0)
                    rolled(act, span, step)

                @block.vector
                def _(dve):
                    def take_x(n, b):
                        if shared:
                            t0 = (first_tile + NT * n) * P
                            dve.wait_ge(x_hi, n + 1)
                            TT(x_view(b, 1), y_t[:, :, t0:t0 + N], x_view(b, 0).bitcast(F32),
                               ALU.subtract).then_inc(x_lo, 1)
                        else:
                            for j in range(XB):
                                dve.wait_ge(x_hi, XB * n + j + 1)
                                w = min(512, DT * N - 512 * j)
                                TT(xt[:, b, 1, 512 * j:512 * j + w], psum[XB0 + (XB * b + j) % 2][:, 0:w],
                                   xt[:, b, 0, 512 * j:512 * j + w].bitcast(F32), ALU.subtract).then_inc(x_lo, 1)

                    def split_hi(n, b, i):
                        dve.wait_ge(w_in[b], 64 * (i + 1))
                        if later(n, 2):
                            dve.wait_ge(d_ps, R * n - R)
                        for r_, h_, l_ in split_pieces(b, egu[:, b], edn[:, b]):
                            V.tensor_copy(h_, r_).then_inc(w_hi, 1)

                    def lo(n, b, j):
                        c0, cw = COLS[j // FT]
                        f = j % FT
                        k = (K * b + j) % 2
                        dve.wait_ge(hh_ready, K * n + j + 1)
                        TT(hid[0:FW[f], b, 1, f, c0:c0 + cw], hf[0:FW[f], k, 0:cw],
                           hid[0:FW[f], b, 0, f, c0:c0 + cw].bitcast(F32), ALU.subtract).then_inc(hl_ready, 1)

                    def step(n, b, i):
                        for j in range(K):
                            f = j % FT
                            cw = COLS[j // FT][1]
                            k = (K * b + j) % 2
                            dve.wait_ge(sg_ready, K * n + j + 1)
                            if later(n, 1) or j >= 2:
                                dve.wait_ge(hl_ready, K * n + j - 1)
                            TT(hf[0:FW[f], k, 0:cw], psum[UB + k][0:FW[f], 0:cw], sg[0:FW[f], k, 0:cw],
                               ALU.mult).then_inc(hf_ready, 1)
                            if j:
                                lo(n, b, j - 1)
                            if j == 1 and not shared and (not isinstance(n, int) or n + 1 < n_units):
                                split_hi(n + 1, 1 - b, i + b)
                        lo(n, b, K - 1)
                        if not isinstance(n, int) or n + 1 < n_units:
                            take_x(n + 1, 1 - b)
                        if shared:
                            for j in range(R):
                                dve.wait_ge(d_ps, R * n + j + 1)
                                ht = h_tok[:, bass.ds(first_tile + NT * n + 2 * j, 2)]
                                TT(ht, psum[DB + (R * b + j) % 2][:].rearrange("p (t d) -> p t d", t=2), ht,
                                   ALU.add).then_inc(d_done, 1)
                        dve_more(dve, extra, n, d_done)

                    if weights_in:
                        dve.wait_ge(w_in[0], 64)
                        for r_, h_, l_ in split_pieces(0, sgu, sdn):
                            V.tensor_copy(h_, r_).then_inc(w_hi, 1)
                    elif not shared:
                        split_hi(0, 0, 0)
                    take_x(0, 0)
                    rolled(dve, span, step, None)

                @block.gpsimd
                def _(pool):
                    if weights_in:
                        for k, (r_, h_, l_) in enumerate(split_pieces(0, sgu, sdn)):
                            pool.wait_ge(w_hi, k + 1)
                            G.tensor_tensor(l_, r_, h_.bitcast(F32), ALU.subtract).then_inc(w_lo, 1)
                    elif shared:
                        pool.nop().then_inc(w_lo, 3)
                        pool.nop().then_inc(w_hi, 3)
                    if not shared:
                        def split_lo(n, b):
                            for k, (r_, h_, l_) in enumerate(split_pieces(b, egu[:, b], edn[:, b])):
                                pool.wait_ge(w_hi, 3 * n + k + 1)
                                G.tensor_tensor(l_, r_, h_.bitcast(F32), ALU.subtract).then_inc(w_lo, 1)

                        def fetch(n, b):
                            if n >= 2:
                                pool.wait_ge(x_ps, XB * (n - 1))
                            for s in range(NS):
                                G.indirect_dma_start(xg[:, b, s], None, y_dram,
                                                     bass.IndirectOffsetOnAxis(ap=slots[:, n, s:s + 1], axis=0)
                                                     ).then_inc(g_in[b], 16)

                        pool.wait_ge(extra["slots_in"], 16)
                        fetch(0, 0)
                        split_lo(0, 0)
                        for n in range(n_units):
                            if n + 1 < n_units:
                                fetch(n + 1, (n + 1) % 2)
                                split_lo(n + 1, (n + 1) % 2)
                    pool_more(pool, extra)

                @block.sync
                def _(sp):
                    if weights_in:
                        load_weights(sp, 0, sw_gate, sw_up, sw_down, w_in[0])
                        sp.wait_ge(w_in[0], 64)
                    if not shared:
                        sp.dma_start(slots[:], table_dram.rearrange("(e p s) o -> p e (s o)", e=E, p=P)
                                     ).then_inc(extra["slots_in"], 16)

                        def fetch_w(n, b):
                            load_weights(sp, b, w_gate[n], w_up[n], w_down[n], w_in[b])

                        fetch_w(0, 0)
                        fetch_w(1, 1)

                        def step(n, b, i):
                            if not isinstance(n, int) or n + 2 < n_units:
                                sp.wait_ge(w_lo, 3 * n + 3)
                                fetch_w(n + 2, b)
                            sp.wait_ge(d_done, R * n + R)
                            sp.dma_start(e_v[n], yb[:]).then_inc(y_out[b], 16)

                        e_v = e_dram.rearrange("(e p s) d -> e p s d", e=E, p=P)
                        rolled(sp, span, step)
                        for b in range(2):
                            sp.wait_ge(y_out[b], 16 * n_units // 2)
                    sp_more(sp, extra)

        none = lambda *a: None

        def scatter(pool, s):
            for t in range(T):
                for k in range(2):
                    G.indirect_dma_start(table_dram, bass.IndirectOffsetOnAxis(ap=slot_to[:, k, t:t + 1], axis=0),
                                         token_id[:, t:t + 1], None, bounds_check=NSLOT - 1,
                                         oob_is_err=False).then_inc(s["scat"], 16)
            pool.wait_ge(s["scat"], 16 * 2 * T)

        phase("sa", True, HALF, (0, HALF, HALF, HALF), 0, ("scat",), none, scatter, none, weights_in=True)
        phase("ex", False, E, (0, 2, E - 2, E), 0, ("slots_in",), none, none, none)

        order = [(t, t % YG) for t in range(T)]

        def gather(pool, s):
            for t, k in order:
                if t >= YG:
                    pool.wait_ge(s["comb"], 2 * (t - YG) + 2)
                for m in range(2):
                    G.indirect_dma_start(yg[:, k, m], None, e_dram,
                                         bass.IndirectOffsetOnAxis(ap=slot_of[:, m, t:t + 1], axis=0)
                                         ).then_inc(s[f"yg{k}"], 16)

        def combine(dve, s, n, d_done):
            def tile(t):
                k = t % YG
                dve.wait_ge(s[f"yg{k}"], 32 * (t // YG + 1))
                ht = h_tok[:, t]
                for m in range(2):
                    STT(out=ht, in0=yg[:, k, m], scalar=gate[:, m, t:t + 1], in1=ht, op0=ALU.mult,
                        op1=ALU.add).then_inc(s["comb"], 1)
                    dve.wait_ge(s["comb"], 2 * t + m + 1)

            for t in range(4 * n, 4 * n + 4):
                tile(t)
            if n == HALF - 1:
                dve.wait_ge(d_done, 2 * HALF)
                for t in range(4 * HALF, T):
                    tile(t)

        def store(sp, s):
            o_v = out.rearrange("c (t p) d -> p (c t) d", p=P)
            for g in range(T // 4):
                sp.wait_ge(s["comb"], 8 * g + 8)
                sp.dma_start(o_v[:, 4 * g:4 * g + 4], h_tok[:, 4 * g:4 * g + 4]).then_inc(s["out_st"], 16)
            sp.wait_ge(s["out_st"], 16 * (T // 4))

        phase("sb", True, HALF, (0, HALF, HALF, HALF), T // 2, [f"yg{k}" for k in range(YG)] + ["comb", "out_st"],
              store, gather, combine)


def vision_tower_block(nc, x, log_dt, inv_A_real, A_imag, B_ri, W_qkv, b_qkv, W_out, b_out, router_w, router_b,
                       w_gate, w_up, w_down, sw_gate, sw_up, sw_down, out):
    C, S, D = out.shape
    E = router_w.shape[1]
    TOPK = 2
    TILES = C * S // P
    CAP = -(-5 * C * S * TOPK // (4 * E))

    h_dram = nc.dram_tensor("h_scratch", [C, S, D], F32).ap()
    y_dram = nc.dram_tensor("y_scratch", [C * S, D], F32).ap()
    table_dram = nc.dram_tensor("table_scratch", [E * CAP, 1], U32).ap()
    e_dram = nc.dram_tensor("expert_rows_scratch", [E * CAP, D], F32).ap()

    with ExitStack() as ctx:
        def sb(name, shape, dt=F32):
            return ctx.enter_context(nc.sbuf_tensor(name, shape, dt))

        psum = [ctx.enter_context(nc.psum_tensor(f"bank{i}", [P, 512], F32)) for i in range(8)]
        ident = sb("ident", [P, P])
        make_tokens(nc, x, log_dt, inv_A_real, A_imag, B_ri, ident, psum, h_dram)

        h_tok = sb("h_tok", [P, TILES, D])
        y_t = sb("y_t", [P, D // P, C * S])
        attend(nc, h_dram, W_qkv, b_qkv, W_out, b_out, ident, psum, h_tok, y_t, y_dram)
        slot_to = sb("slot_to", [P, TOPK, TILES], U32)
        slot_of = sb("slot_of", [P, TOPK, TILES], U32)
        gate = sb("gate", [P, TOPK, TILES])
        token_id = sb("token_id", [P, TILES], U32)
        route(nc, router_w, router_b, ident, psum, y_t, slot_to, slot_of, gate, token_id, table_dram, CAP)
        experts(nc, (w_gate, w_up, w_down, sw_gate, sw_up, sw_down), ident, psum, h_tok, y_t, y_dram, slot_to,
                slot_of, gate, token_id, table_dram, e_dram, out, CAP)


_INS = ['x', 'L0_tok_log_dt', 'L0_tok_inv_A_real', 'L0_tok_A_imag', 'L0_tok_B_ri', 'L0_attn_W_qkv', 'L0_attn_b_qkv',
        'L0_attn_W_out', 'L0_attn_b_out', 'L0_ffn_router_w', 'L0_ffn_router_b', 'L0_ffn_w_gate', 'L0_ffn_w_up',
        'L0_ffn_w_down', 'L0_ffn_sw_gate', 'L0_ffn_sw_up', 'L0_ffn_sw_down']
_OUTS = [((16, 256, 256), 'float32')]


def kernel(**inputs):
    import numpy as _np
    import concourse.bacc as _bacc
    from concourse import mybir as _mybir
    from concourse.bass_utils import run_bass_kernel_spmd as _run

    nc = _bacc.Bacc("TRN2", target_bir_lowering=False, num_devices=1)
    arrays, args = {}, []
    for name in _INS:
        a = _np.ascontiguousarray(inputs[name])
        arrays[f"in_{name}_dram"] = a
        args.append(nc.dram_tensor(f"in_{name}_dram", a.shape, _mybir.dt.from_np(a.dtype), kind="ExternalInput").ap())
    for i, (shape, dtype) in enumerate(_OUTS):
        dt = _mybir.dt.from_np(_np.dtype(dtype))
        args.append(nc.dram_tensor(f"out_{i}_dram", shape, dt, kind="ExternalOutput").ap())
    vision_tower_block(nc, *args)
    r = _run(nc, [arrays], core_ids=[0])
    return r.results[0]["out_0_dram"]
```

```python
import math
from contextlib import ExitStack

import concourse.bass as bass
from concourse import mybir

ALU = mybir.AluOpType
ACT = mybir.ActivationFunctionType
AX = mybir.AxisListType
F32 = mybir.dt.float32
F32R = mybir.dt.float32r
I32 = mybir.dt.int32
U32 = mybir.dt.uint32

P = 128


class Chain:

    def __init__(self, eng, sem):
        self.eng, self.sem, self.base, self.k = eng, sem, 0, 0

    def link(self, ins):
        self.k += 1
        ins.then_inc(self.sem, 1)
        self.eng.wait_ge(self.sem, self.base + self.k)

    def tick(self, ins):
        self.k += 1
        ins.then_inc(self.sem, 1)

    def start(self, base):
        self.base, self.k = base, 0


def rolled(eng, span, step, chain=None):
    first, lo, hi, last = span
    per = 0

    def written_out(steps):
        nonlocal per
        for n in steps:
            if chain:
                chain.start(chain.base + chain.k)
            step(n, n % 2, n // 2)
            per = chain.k if chain else 0

    written_out(range(first, lo))
    base = chain.base + chain.k if chain else 0
    if lo == hi:
        return written_out(range(hi, last))
    with eng.Fori(lo // 2, hi // 2) as i:
        for b in range(2):
            if chain:
                chain.start(base + per * (2 * i + b - lo))
            step(2 * i + b, b, i)
            assert not chain or chain.k == per
    if chain:
        chain.start(base + per * (hi - lo))
    written_out(range(hi, last))


def make_tokens(nc, x, log_dt, inv_A_real, A_imag, B_ri, ident, psum, h_dram, weights):
    C, S, N, _ = x.shape
    J = S // 2
    GP = 16
    NG = J // GP
    LB = 128
    A = 2
    QG = GP // 2
    KP = 8
    SPLIT = 9
    NCB = C // 2
    TT = nc.vector.tensor_tensor

    with ExitStack() as ctx:
        def sb(name, shape, dt=F32):
            return ctx.enter_context(nc.sbuf_tensor(name, shape, dt))

        def sem(name):
            return ctx.enter_context(nc.semaphore(name))

        x_rows = sb("x_rows", [P, C, 256])
        ldt = sb("ldt", [P, 2])
        dt = sb("dt", [P, 2])
        a_raw = sb("a_raw", [P, P])
        a_exp = sb("a_exp", [P, P])
        e_base = sb("e_base", [P, 2])
        a_im = sb("a_im", [P, P])
        b_rows = sb("b_rows", [P, 256])
        wr = sb("wr", [P, P])
        wi = sb("wi", [P, P])
        tmp = sb("tmp", [P, 6, P])
        z_rows = sb("z_rows", [P, KP, 2, P])
        z_re = sb("z_re", [P, KP, J])
        z_im = sb("z_im", [P, KP, 2, J])
        b_re = sb("b_re", [P, J])
        b_im = sb("b_im", [P, 2, J])
        c_t = sb("c_t", [P, 2, C, J])
        g_cmp = sb("g_cmp", [P, 2, A, 2, C, GP])
        g_t = sb("g_t", [P, 2, C, GP])
        g_u = sb("g_u", [P, 2, C, GP])
        g_blk = sb("g_blk", [P, 2, 2, GP, 2, A, C])
        w_pow = sb("w_pow", [P, 2, 2, GP, LB])
        w_t = sb("w_t", [P, 2, GP, LB // 2])
        w_u = sb("w_u", [P, 2, GP, LB // 2])
        h_out = sb("h_out", [P, 2, 2, 512])

        ident_ready = sem("ident_ready")
        par_loaded = sem("par_loaded")
        x_loaded = sem("x_loaded")
        exp_ready = sem("exp_ready")
        dve_chain = sem("dve_chain1")
        pool_chain = sem("pool_chain1")
        z_ready = sem("z_ready")
        tr_ready = sem("tr_ready")
        tr_copied = sem("tr_copied")
        const_ready = sem("const_ready")
        g_ready = sem("g_ready")
        blk_ready = sem("blk_ready")
        w_low = sem("w_low")
        w_dve = sem("w_dve")
        w_pool = sem("w_pool")
        prod_ready = sem("prod_ready")
        out_ready = sem("out_ready")
        stored = [sem(f"stored{b}") for b in range(2)]

        x_v = x.rearrange("c (j s) n r -> j c (s n r)", s=2)
        h_v = h_dram.rearrange("c (q j s) (a b) -> j s a c q b", j=2, s=2, a=A)
        TR_C, TR_Z = NCB, NCB + 1 + KP // 2
        CP_C, CP_B = NCB, NCB + 3

        block = ctx.enter_context(nc.Block())

        @block.sync
        def _(sp):
            sp.dma_start(ldt[:], log_dt.rearrange("(j s) -> j s", s=2)).then_inc(par_loaded, 16)
            sp.dma_start(a_raw[:], inv_A_real.rearrange("(j s) n -> j (s n)", s=2)).then_inc(par_loaded, 16)
            sp.dma_start(a_im[:], A_imag.rearrange("(j s) n -> j (s n)", s=2)).then_inc(par_loaded, 16)
            sp.dma_start(b_rows[:], B_ri.rearrange("(j s) n r -> j (s n r)", s=2)).then_inc(par_loaded, 16)
            for k in range(4):
                sp.dma_start(x_rows[:, 4 * k:4 * k + 4], x_v[:, 4 * k:4 * k + 4]).then_inc(x_loaded, 16)

            weights.load(sp)

            def store(g, b, i):
                sp.wait_ge(out_ready, 2 * g + 2)
                for j in range(2):
                    for s in range(2):
                        for a in range(A):
                            p0 = 64 * j + 32 * s + 16 * a
                            sp.dma_start(h_v[j, s, a][:, bass.ts(g, QG), :],
                                         h_out[p0:p0 + C, b].rearrange("c k (q b) -> c (k q) b", b=LB)
                                         ).then_inc(stored[b], 16)

            rolled(sp, (0, 0, NG, NG), store)
            for b in range(2):
                sp.wait_ge(stored[b], 64 * NG)

        @block.scalar
        def _(act):
            act.wait_ge(par_loaded, 64)
            nc.scalar.activation(a_exp[:], a_raw[:], ACT.Exp).then_inc(exp_ready, 1)
            for n in range(NCB):
                act.wait_ge(tr_ready, n + 1)
                nc.scalar.activation(c_t[:, :, 2 * n:2 * n + 2, :].rearrange("p r c j -> p c r j"),
                                     psum[n % 4][:].rearrange("p (c r j) -> p c r j", c=2, r=2),
                                     ACT.Copy).then_inc(tr_copied, 1)
            act.wait_ge(tr_ready, NCB + 1)
            bank = psum[NCB % 4]
            nc.scalar.activation(b_re[:], bank[:, 0:J], ACT.Copy, scale=2.0).then_inc(tr_copied, 1)
            nc.scalar.activation(b_im[:, 0], bank[:, J:2 * J], ACT.Copy, scale=2.0).then_inc(tr_copied, 1)
            nc.scalar.activation(b_im[:, 1], bank[:, J:2 * J], ACT.Copy, scale=-2.0).then_inc(tr_copied, 1)
            for q in range(KP // 2):
                act.wait_ge(tr_ready, NCB + 2 + q)
                v = psum[(NCB + 1 + q) % 4][:].rearrange("p (k r j) -> p k r j", k=2, r=2)
                k2 = slice(2 * q, 2 * q + 2)
                nc.scalar.activation(z_re[:, k2], v[:, :, 0], ACT.Copy).then_inc(tr_copied, 1)
                nc.scalar.activation(z_im[:, k2, 0], v[:, :, 1], ACT.Copy).then_inc(tr_copied, 1)
                nc.scalar.activation(z_im[:, k2, 1], v[:, :, 1], ACT.Copy, scale=-1.0).then_inc(tr_copied, 1)
            act.wait_ge(const_ready, 3)

            def lay_out(g, b):
                act.wait_ge(g_ready, 2 * g + 2)
                if not (isinstance(g, int) and g < 2):
                    act.wait_ge(prod_ready, g - 1)
                for r in range(2):
                    for s in range(2):
                        src = g_cmp[64 * s:64 * s + 64, b, :, r].rearrange("p a c j -> p j a c")
                        nc.scalar.activation(g_blk[64 * s:64 * s + 64, b, r, :, s], src, ACT.Copy,
                                             scale=-1.0 if r else 1.0).then_inc(blk_ready, 1)

            def copy_out(g, b, i):
                act.wait_ge(prod_ready, g + 1)
                if not (isinstance(g, int) and g < 2):
                    act.wait_ge(stored[b], 128 * i)
                for k in range(2):
                    nc.scalar.activation(h_out[:, b, k], psum[2 * b + k][:], ACT.Copy).then_inc(out_ready, 1)

            def step(n, b, i):
                lay_out(n, b)
                if not (isinstance(n, int) and n < 1):
                    copy_out(n - 1, 1 - b, i + b - 1)

            rolled(act, (0, 2, NG, NG), step)
            copy_out(NG - 1, (NG - 1) % 2, (NG - 1) // 2)

        @block.vector
        def _(dve):
            ch = Chain(dve, dve_chain)
            link = ch.link
            nc.vector.memset(w_pow[:, :, 0, :, 0:1], 1.0).then_inc(const_ready, 1)
            nc.vector.memset(w_pow[:, :, 1, :, 0:1], 0.0).then_inc(const_ready, 1)
            dve.wait_ge(exp_ready, 2)
            for s in range(2):
                h = slice(64 * s, 64 * s + 64)
                nc.vector.tensor_scalar(wr[:, h], a_exp[:, h], dt[:, s:s + 1], -0.5, ALU.mult,
                                        ALU.mult).then_inc(dve_chain, 1)
                nc.vector.tensor_scalar(wi[:, h], a_im[:, h], dt[:, s:s + 1], 0.5, ALU.mult,
                                        ALU.mult).then_inc(dve_chain, 1)
            ch.k = 4
            dve.wait_ge(dve_chain, 4)
            t = [tmp[:, i] for i in range(6)]
            zr, zi = z_rows[:, 0, 0], z_rows[:, 0, 1]
            ch.tick(nc.vector.tensor_scalar(t[0], wr[:], -1.0, 1.0, ALU.mult, ALU.add))
            ch.tick(nc.vector.tensor_scalar(t[1], wr[:], 1.0, None, ALU.add))
            link(TT(t[2], wi[:], wi[:], ALU.mult))
            ch.tick(TT(t[1], t[0], t[1], ALU.mult))
            link(TT(t[3], t[0], t[0], ALU.mult))
            link(TT(t[3], t[3], t[2], ALU.add))
            link(nc.vector.reciprocal(t[4], t[3]))
            link(TT(t[1], t[1], t[2], ALU.subtract))
            link(TT(zr, t[1], t[4], ALU.mult))
            link(nc.vector.scalar_tensor_tensor(out=zi, in0=wi[:], scalar=2.0, in1=t[4], op0=ALU.mult, op1=ALU.mult))
            for k in range(1, KP):
                r0, i0 = z_rows[:, k - 1, 0], z_rows[:, k - 1, 1]
                ch.tick(TT(t[0], r0, r0, ALU.mult))
                ch.tick(TT(t[1], i0, i0, ALU.mult))
                link(nc.vector.scalar_tensor_tensor(out=z_rows[:, k, 1], in0=r0, scalar=2.0, in1=i0,
                                                    op0=ALU.mult, op1=ALU.mult))
                last = TT(z_rows[:, k, 0], t[0], t[1], ALU.subtract)
                link(last)
                if k % 2:
                    dve.nop().then_inc(z_ready, 1)
            dve.wait_ge(tr_copied, CP_B + 3 * (KP // 2))

            def step(g, b, i):
                if not (isinstance(g, int) and g < 2):
                    dve.wait_ge(prod_ready, g - 1)
                js = bass.ts(g, GP)
                w = w_pow[:, b]
                ch.tick(nc.vector.tensor_copy(w[:, 0, :, 1], z_re[:, 0, js]))
                link(nc.vector.tensor_copy(w[:, 1, :, 1], z_im[:, 0, 0, js]))
                for k in range(1, KP - 1):
                    m = 1 << k
                    n = SPLIT if k == KP - 2 else GP
                    if k == KP - 2:
                        dve.nop().then_inc(w_low, 1)
                    jn = bass.ds(g * GP, n)
                    zr = z_re[:, k, jn].unsqueeze(1).unsqueeze(3).to_broadcast([P, 2, n, m])
                    zi = z_im[:, k, :, jn].unsqueeze(3).to_broadcast([P, 2, n, m])
                    wt, wu = w_t[:, :, 0:n, 0:m], w_u[:, :, 0:n, 0:m]
                    ch.tick(TT(wt, w[:, :, 0:n, 0:m], zr, ALU.mult))
                    link(TT(wu, w[:, :, 0:n, 0:m], zi, ALU.mult))
                    link(TT(w[:, :, 0:n, m:2 * m], wt, w_u[:, ::-1, 0:n, 0:m], ALU.add))
                dve.nop().then_inc(w_dve, 1)

            rolled(dve, (0, 2, NG, NG), step, ch)
            weights.split(dve, psum[4])

        @block.gpsimd
        def _(pool):
            ch = Chain(pool, pool_chain)
            link = ch.link
            GT = nc.gpsimd.tensor_tensor
            link(nc.gpsimd.memset(e_base[:], math.e))
            pool.wait_ge(par_loaded, 64)
            GT(dt[:], e_base[:], ldt[:], ALU.pow).then_inc(exp_ready, 1)
            link(nc.gpsimd.memset(ident[:], 0.0))
            nc.gpsimd.affine_select(out=ident[:], in_=ident[:], compare_op=ALU.not_equal, fill=1.0, base=0,
                                    pattern=[[-1, P]], channel_multiplier=1).then_inc(ident_ready, 1)
            nc.gpsimd.memset(g_blk[:], 0.0).then_inc(const_ready, 1)
            pt = sb("pt", [P, 2, GP - SPLIT, LB // 2])
            pu = sb("pu", [P, 2, GP - SPLIT, LB // 2])
            pool.wait_ge(tr_copied, CP_B + 3 * (KP // 2))

            def step(g, b, i):
                js = bass.ts(g, GP)
                if not (isinstance(g, int) and g < 2):
                    pool.wait_ge(blk_ready, 4 * g - 4)
                shape = [P, 2, C, GP]
                br = b_re[:, js].unsqueeze(1).unsqueeze(1).to_broadcast(shape)
                bi = b_im[:, :, js].unsqueeze(2).to_broadcast(shape)
                zr = z_re[:, KP - 1, js].unsqueeze(1).unsqueeze(1).to_broadcast(shape)
                zi = z_im[:, KP - 1, :, js].unsqueeze(2).to_broadcast(shape)
                for a, (src, fr, fi) in enumerate(((c_t[:, :, :, js], br, bi), (g_cmp[:, b, 0], zr, zi))):
                    ch.tick(GT(g_t[:], src, fr, ALU.mult))
                    link(GT(g_u[:], src, fi, ALU.mult))
                    last = GT(g_cmp[:, b, a], g_t[:], g_u[:, ::-1], ALU.add)
                    link(last)
                    pool.nop().then_inc(g_ready, 1)
                pool.wait_ge(w_low, g + 1)
                k, m, n = KP - 2, LB // 2, GP - SPLIT
                w = w_pow[:, b]
                jn = bass.ds(g * GP + SPLIT, n)
                zr = z_re[:, k, jn].unsqueeze(1).unsqueeze(3).to_broadcast([P, 2, n, m])
                zi = z_im[:, k, :, jn].unsqueeze(3).to_broadcast([P, 2, n, m])
                ch.tick(GT(pt[:], w[:, :, SPLIT:GP, 0:m], zr, ALU.mult))
                link(GT(pu[:], w[:, :, SPLIT:GP, 0:m], zi, ALU.mult))
                link(GT(w[:, :, SPLIT:GP, m:2 * m], pt[:], pu[:, ::-1], ALU.add))
                pool.nop().then_inc(w_pool, 1)

            rolled(pool, (0, 2, NG, NG), step, ch)

        @block.tensor
        def _(pe):
            pe.wait_ge(ident_ready, 1)
            pe.wait_ge(x_loaded, 64)
            for n in range(NCB):
                if n >= 4:
                    pe.wait_ge(tr_copied, n - 3)
                for c in range(2):
                    for r in range(2):
                        q = 2 * c + r
                        src = x_rows[:, 2 * n + c].rearrange("j (m r) -> j r m", r=2)[:, r]
                        last = nc.tensor.transpose(psum[n % 4][:, q * J:(q + 1) * J], src, ident[:])
                last.then_inc(tr_ready, 1)
            pe.wait_ge(par_loaded, 64)
            pe.wait_ge(tr_copied, NCB - 3)
            for r in range(2):
                src = b_rows[:].rearrange("j (m r) -> j r m", r=2)[:, r]
                last = nc.tensor.transpose(psum[NCB % 4][:, r * J:(r + 1) * J], src, ident[:])
            last.then_inc(tr_ready, 1)
            for q in range(KP // 2):
                pe.wait_ge(z_ready, q + 1)
                pe.wait_ge(tr_copied, NCB - 2 + q if q < 3 else CP_B)
                for k in range(2):
                    for r in range(2):
                        i = 2 * k + r
                        last = nc.tensor.transpose(psum[(NCB + 1 + q) % 4][:, i * J:(i + 1) * J],
                                                   z_rows[:, 2 * q + k, r], ident[:])
                last.then_inc(tr_ready, 1)
            pe.wait_ge(tr_copied, CP_B + 3 * (KP // 2))
            pe.wait_ge(const_ready, 3)

            def step(g, b, i):
                pe.wait_ge(blk_ready, 4 * g + 4)
                pe.wait_ge(w_dve, g + 1)
                pe.wait_ge(w_pool, g + 1)
                if not (isinstance(g, int) and g < 2):
                    pe.wait_ge(out_ready, 2 * g - 2)
                for q in range(QG):
                    bank, col = psum[2 * b + q // 4], (q % 4) * LB
                    for r in range(2):
                        for j in range(2):
                            last = nc.tensor.matmul(bank[64 * j:64 * j + 64, col:col + LB],
                                                    g_blk[:, b, r, 2 * q + j].rearrange("p s a c -> p (s a c)"),
                                                    w_pow[:, b, r, 2 * q + j], start=(r == 0), stop=(r == 1),
                                                    tile_position=(0, 64 * j))
                last.then_inc(prod_ready, 1)

            rolled(pe, (0, 2, NG, NG), step)
            weights.bias_product(pe, psum[4])


class AttentionWeights:

    def __init__(self, ctx, nc, W_qkv, b_qkv, W_out, b_out):
        def sb(name, shape, dt=F32):
            return ctx.enter_context(nc.sbuf_tensor(name, shape, dt))

        self.nc = nc
        self.dram = W_qkv, b_qkv, W_out, b_out
        D = W_out.shape[0]
        NH, DH = 16, 16
        DT = D // P
        self.D, self.DT, self.DH, self.H8 = D, DT, DH, NH // 2
        self.pr = sb("pr", [P, 8, 2, D])
        spare = self.pr[:].rearrange("p b t s -> p (b t s)")
        self.qkv_raw = spare[:, 0:6 * D].rearrange("p (t n) -> p t n", t=DT)
        self.wo_raw = spare[:, 6 * D:8 * D].rearrange("p (t n) -> p t n", t=DT)
        self.bv_cols = spare[:, 8 * D:8 * D + DT * P].rearrange("p (t n) -> p t n", t=DT)
        self.bo_rows = spare[:, 10 * D:11 * D]
        self.wqk = sb("wqk", [P, 2, DT, 4, DH, self.H8], F32R)
        self.wv = sb("wv", [P, 2, DT, D], F32R)
        self.wo = sb("wo", [P, 2, DT, D], F32R)
        self.bqk = sb("bqk", [P, 4])
        self.bv = sb("bv", [P, DT])
        self.bias_rows = sb("bias_rows", [P, D])
        self.loaded, self.high, self.cols_ready, self.bias_ps = (
            ctx.enter_context(nc.semaphore(n)) for n in ("w_loaded", "w_high", "bv_cols_ready", "bias_ps"))

    def load(self, sp):
        W_qkv, b_qkv, W_out, b_out = self.dram
        D = self.D

        def wl(dst, src, slow=False):
            sp.dma_start(dst, src, allow_slow_non_contiguous=slow).then_inc(self.loaded, 16)

        wl(self.qkv_raw, W_qkv.rearrange("(t p) n -> p t n", p=P))
        wl(self.wo_raw, W_out.rearrange("(t p) n -> p t n", p=P))
        for x in range(4):
            wl(self.bqk[:, x:x + 1], b_qkv[x * P:(x + 1) * P].rearrange("(h r) -> r h", r=self.DH), slow=True)
        wl(self.bv[:], b_qkv[2 * D:3 * D].rearrange("(t p) -> p t", p=P), slow=True)
        wl(self.bo_rows, b_out.partition_broadcast(P))

    def split(self, dve, bank):
        V, D = self.nc.vector, self.D
        dve.wait_ge(self.loaded, 128)
        pairs = [(self.qkv_raw[:, dt, 0:2 * D].rearrange("p (x h r) -> p x h r", x=4, h=self.H8),
                  [self.wqk[:, part, dt].rearrange("p x r h -> p x h r") for part in range(2)])
                 for dt in range(self.DT)]
        pairs += [(self.qkv_raw[:, :, 2 * D:3 * D], [self.wv[:, 0], self.wv[:, 1]]),
                  (self.wo_raw, [self.wo[:, 0], self.wo[:, 1]])]
        for whole, (high, low) in pairs:
            V.tensor_copy(high, whole).then_inc(self.high, 1)
        V.memset(self.bv_cols, 1.0).then_inc(self.high, 1)
        dve.wait_ge(self.high, len(pairs) + 1)
        for dt in range(self.DT):
            V.tensor_scalar(self.bv_cols[:, dt], self.bv_cols[:, dt], self.bv[:, dt:dt + 1], None,
                            ALU.mult).then_inc(self.cols_ready, 1)
        for whole, (high, low) in pairs:
            V.tensor_tensor(low, whole, high.bitcast(F32), ALU.subtract)
        dve.wait_ge(self.bias_ps, 1)
        V.tensor_tensor(self.bias_rows[:], bank[:, 0:D], self.bo_rows, ALU.add)

    def bias_product(self, pe, bank):
        pe.wait_ge(self.cols_ready, self.DT)
        for dt in range(self.DT):
            last = self.nc.tensor.matmul(bank[:, 0:self.D], self.bv_cols[:, dt], self.wo_raw[:, dt],
                                         start=(dt == 0), stop=(dt == self.DT - 1))
        last.then_inc(self.bias_ps, 1)




def attend(nc, h_dram, weights, ident, psum, h_tok, y_t, y_dram):
    C, S, D = h_dram.shape
    NH, DH = 16, 16
    SCALE = 1.0 / DH ** 0.5
    QT = S // P
    DT = D // P
    H8 = NH // 2
    ZERO, MROW, KROWS = 64, 96, 98
    EPS = 1e-5
    GH = 4
    PBUF = 8
    S2B, POB, X, Y, SA, SB = 0, 2, 4, 5, 6, 7
    TT, TS, STT = nc.vector.tensor_tensor, nc.vector.tensor_scalar, nc.vector.scalar_tensor_tensor
    mm = nc.tensor.matmul
    SPAN = (-2, 2, C - 4, C + 2)

    with ExitStack() as ctx:
        def sb(name, shape, dt=F32):
            return ctx.enter_context(nc.sbuf_tensor(name, shape, dt))

        def sem(name):
            return ctx.enter_context(nc.semaphore(name))

        def sems(name, n):
            return [sem(f"{name}{i}") for i in range(n)]

        pr, wqk, wv, wo, bqk, bias_rows = (weights.pr, weights.wqk, weights.wv, weights.wo, weights.bqk,
                                           weights.bias_rows)
        xn = sb("xn", [P, QT, D])
        xt = sb("xt", [P, 2, 2, DT, S], F32R)
        qk = sb("qk", [P, 2, 2, 2, 2, S], F32R)
        qs = sb("qs", [P, 2, NH, S], F32R)
        ks = sb("ks", [P, 2, NH, S], F32R)
        mx = sb("mx", [P, QT, NH])
        mp = sb("mp", [H8, 2, S], F32R)
        va = sb("va", [P, 2, QT, NH, 32])
        o_sb = sb("o_sb", [P, 4, S])
        den = sb("den", [P, NH])
        on = xn
        ot = sb("ot", [P, 2, DT, S], F32R)
        y = o_sb[:, QT:2 * QT]
        bn = sb("bn", [P, 2, QT, 6])
        mv = sb("mv", [P, 2, QT, 2])
        vare = sb("vare", [P, 2, QT])
        rstd = sb("rstd", [P, 2, QT])
        half = sb("half", [P, QT])
        eps = sb("eps", [P, QT])

        h_first = sem("h_first")
        h_loaded = sems("h_loaded", 4)
        pool_const = sem("pool_const")
        zeroed = sem("zeroed")
        dve_chain, pool_chain = sem("dve_chain2"), sem("pool_chain2")
        centred = sems("centred", 2)
        ln1_stat, xn_ready, hb = sem("ln1_stat"), sem("xn_ready"), sem("hb")
        xt_ps, xt_hi, xt_lo = sem("xt_ps"), sem("xt_hi"), sem("xt_lo")
        q_ps, q_hi, q_lo = sem("q_ps"), sem("q_hi"), sem("q_lo")
        k_ps, k_hi, k_lo = sem("k_ps"), sem("k_hi"), sem("k_lo")
        v_ps, v_ready = sem("v_ps"), sem("v_ready")
        stk = [sems(f"stk{b}", 2) for b in range(2)]
        mrow = [sems(f"mrow{b}", 2) for b in range(2)]
        s1_ps, s1_max = sem("s1_ps"), sem("s1_max")
        mt_ps, m_hi, m_lo = sem("mt_ps"), sem("m_hi"), sem("m_lo")
        s2_ps, p_ready, pv_done, o_ready = sem("s2_ps"), sem("p_ready"), sem("pv_done"), sem("o_ready")
        ot_ps, on_ready = sem("ot_ps"), sem("on_ready")
        ont_ps, ont_hi, ont_lo = sem("ont_ps"), sem("ont_hi"), sem("ont_lo")
        pj_ps, h1_ready, ln2_stat, y_ready = sem("pj_ps"), sem("h1_ready"), sem("ln2_stat"), sem("y_ready")
        r_done, yt_ps, yt_ready = sem("r_done"), sem("yt_ps"), sem("yt_ready")
        y_stored = sem("y_stored")

        def has(c):
            if not isinstance(c, int):
                return (True,) * 6
            return c + 3 < C, c + 2 < C, 0 <= c + 1 < C, 0 <= c < C, 0 <= c - 1 < C, 0 <= c - 2 < C

        def later(c, n):
            return not isinstance(c, int) or c >= n

        def first(eng, *counts):
            counts = [n if isinstance(n, int) or n is None else eng.compute_val(n) for n in counts]
            eng.wait_ge(h_loaded[0], 16)
            return counts

        def toks(c):
            return bass.ts(c, S)

        def tiles(c):
            return bass.ts(c, QT)

        block = ctx.enter_context(nc.Block())

        @block.sync
        def _(sp):
            h_v = h_dram.rearrange("c (t p) d -> p (c t) d", p=P)
            n = C * QT // 4
            sp.dma_start(h_tok[:, 0:QT], h_v[:, 0:QT]).then_inc(h_first, 16)
            sp.dma_start(h_tok[:, QT:n], h_v[:, QT:n]).then_inc(h_loaded[0], 16)
            for k in range(1, 4):
                sp.dma_start(h_tok[:, n * k:n * (k + 1)], h_v[:, n * k:n * (k + 1)]).then_inc(h_loaded[k], 16)

            def stack(a, b, s, used):
                made, used = first(sp, 2 * a + 2, used)
                for done in (q_hi, q_lo, k_hi, k_lo):
                    sp.wait_ge(done, made)
                if used is not None:
                    sp.wait_ge(s2_ps, used)
                for t, which, parts in ((qs, 0, (0, 0, 1, 1)), (ks, 1, (0, 1, 0, 1))):
                    for slot, part in enumerate(parts):
                        sp.dma_start(t[16 * slot:16 * slot + 16, b, H8 * s:H8 * s + H8].bitcast(F32),
                                     qk[:, b, which, part, s].bitcast(F32)).then_inc(stk[b][s], 16)

            def max_rows(n, b, s):
                made, used = first(sp, 2 * n + s + 1, 16 * n - 16 if later(n, 2) else None)
                sp.wait_ge(m_hi, made)
                sp.wait_ge(m_lo, made)
                if used is not None:
                    sp.wait_ge(s2_ps, used)
                for part in range(2):
                    sp.dma_start(qs[MROW + part:MROW + part + 1, b, H8 * s:H8 * s + H8].bitcast(F32),
                                 mp[:, part].bitcast(F32)).then_inc(mrow[b][s], 16)

            def step(c, b, i):
                ln, A, B, Cc, end, fin = has(c)
                if B:
                    stack(c + 1, 1 - b, 1, 16 * c if later(c, 1) else None)
                if Cc:
                    max_rows(c, b, 1)
                if A:
                    stack(c + 2, b, 0, 16 * c + 8 if later(c, 0) else None)
                if fin:
                    u = c - 2
                    made, = first(sp, u + 1)
                    sp.wait_ge(y_ready, made)
                    sp.dma_start(y_dram[toks(u), :].rearrange("(t p) d -> p t d", p=P),
                                 y).then_inc(y_stored, 16)
                if B:
                    max_rows(c + 1, 1 - b, 0)

            rolled(sp, SPAN, step)
            sp.wait_ge(y_stored, 16 * C)

        @block.gpsimd
        def _(pool):
            ch = Chain(pool, pool_chain)
            link = ch.link
            GT = nc.gpsimd.tensor_tensor
            def fill(n, at, value):
                if n:
                    pool.wait_ge(pool_const, n)
                nc.gpsimd.memset(at, value).then_inc(pool_const, 1)

            fill(0, half[:], -0.5)
            fill(1, eps[:], EPS)
            pool.wait_ge(pool_const, 2)

            def power(which, stat, n):
                pool.wait_ge(stat, n)
                link(GT(vare[:, which], mv[:, which, :, 1], eps[:], ALU.add))
                link(GT(rstd[:, which], vare[:, which], half[:], ALU.pow))

            def normal(which, out, n, done):
                shape = [P, QT, D]
                GT(out, h_tok[:, tiles(n)], mv[:, which, :, 0:1].to_broadcast(shape),
                   ALU.subtract).then_inc(centred[which], 1)
                pool.wait_ge(centred[which], n + 1)
                GT(out, out, rstd[:, which].unsqueeze(2).to_broadcast(shape), ALU.mult).then_inc(done, 1)

            def add_bias(n):
                ht = h_tok[:, tiles(n)]
                GT(ht, ht, bias_rows[:].unsqueeze(1).to_broadcast([P, QT, D]), ALU.add).then_inc(hb, 1)

            power(0, ln1_stat, 1)
            normal(0, xn[:], 0, xn_ready)
            add_bias(0)
            pool.wait_ge(hb, 1)
            fill(2, ks[MROW:KROWS].bitcast(F32), 1.0)
            fill(3, va[:], 0.0)
            fill(4, va[:, :, :, :, DH:DH + 1], 1.0)
            pool.wait_ge(pool_const, 5)

            def step(c, b, i):
                ln, A, B, Cc, end, fin = has(c)
                if ln:
                    power(0, ln1_stat, c + 4)
                if fin:
                    u = c - 2
                    o_left, stored, used = first(pool, 2 * c, 16 * u, u)
                    if end:
                        pool.wait_ge(ot_ps, o_left)
                    if later(u, 1):
                        pool.wait_ge(y_stored, stored)
                        pool.wait_ge(yt_ps, used)
                    normal(1, y, u, y_ready)
                    made, = first(pool, u + 1)
                    pool.wait_ge(y_ready, made)
                    GT(h_tok[:, tiles(u)], h_tok[:, tiles(u)], y, ALU.add).then_inc(r_done, 1)
                if ln:
                    x_left, o_left = first(pool, c + 3, c)
                    pool.wait_ge(xt_ps, x_left)
                    if end:
                        pool.wait_ge(ont_ps, o_left)
                    normal(0, xn[:], c + 3, xn_ready)
                    add_bias(c + 3)
                if end:
                    power(1, ln2_stat, c)

            rolled(pool, SPAN, step, ch)

        @block.scalar
        def _(act):
            A_ = nc.scalar.activation
            act.wait_ge(pool_const, 2)
            A_(ks[ZERO:MROW], eps[ZERO:MROW, 0:1].unsqueeze(1).unsqueeze(1).to_broadcast([MROW - ZERO, 2, NH, S]),
               ACT.Copy, scale=0.0).then_inc(zeroed, 1)

            def step(c, b, i):
                ln, A, B, Cc, end, fin = has(c)
                a, d, t, u = c + 2, c + 1, c - 1, c - 2

                def max_hi(n, s):
                    act.wait_ge(mt_ps, 2 * n + s + 1)
                    if s or Cc:
                        act.wait_ge(mrow[b][1 - s], 32 * (i + 1))
                    A_(mp[:, 0], psum[(Y, X)[s]][0:H8, 0:S], ACT.Copy, scale=-1.0).then_inc(m_hi, 1)

                def parts_hi(which, bank, ps, hi):
                    act.wait_ge(ps, a + 1)
                    for s in range(2):
                        A_(qk[:, b, which, 0, s], psum[bank][:, s * S:(s + 1) * S], ACT.Identity,
                           bias=bqk[:, 2 * which + s:2 * which + s + 1]).then_inc(hi, 1)

                def o_copy(n, k):
                    act.wait_ge(pv_done, 4 * n + 2 * k + 2)
                    if later(n, 1):
                        act.wait_ge(ot_ps, 2 * n)
                    A_(o_sb[:, 2 * k:2 * k + 2].rearrange("p g s -> p (g s)"), psum[POB + k][:],
                       ACT.Copy).then_inc(o_ready, 1)

                for h in range(NH):
                    if h == 1 and A:
                        act.wait_ge(xt_ps, a + 1)
                        A_(xt[:, b, 0].rearrange("p t s -> p (t s)"), psum[Y][:], ACT.Copy).then_inc(xt_hi, 1)
                    if h == 2 and Cc:
                        max_hi(c, 1)
                    if h == 3 and end:
                        if later(u, 1):
                            act.wait_ge(y_stored, 16 * u)
                            act.wait_ge(r_done, u)
                            act.wait_ge(yt_ps, u)
                        o_copy(t, 1)
                    if h == 4 and A:
                        if later(c, 0):
                            act.wait_ge(stk[b][0], 128 * (i + 1))
                            act.wait_ge(stk[b][1], 128 * (i + 1))
                        parts_hi(0, X, q_ps, q_hi)
                    if h == 5 and A:
                        parts_hi(1, Y, k_ps, k_hi)
                    if h == 14 and fin:
                        act.wait_ge(yt_ps, u + 1)
                        A_(y_t[:, :, toks(u)], psum[X][:].rearrange("p (t s) -> p t s", t=DT),
                           ACT.Copy).then_inc(yt_ready, 1)
                    if h == 10 and B:
                        max_hi(d, 0)
                    if h == 11 and Cc:
                        o_copy(c, 0)
                    if h == 12 and end:
                        act.wait_ge(ont_ps, t + 1)
                        if later(t, 1):
                            act.wait_ge(pj_ps, t)
                        A_(ot[:, 0].rearrange("p t s -> p (t s)"), psum[X][:], ACT.Copy).then_inc(ont_hi, 1)
                    if Cc:
                        act.wait_ge(s2_ps, 16 * c + h + 1)
                        if h >= PBUF or later(c, 1):
                            act.wait_ge(pv_done, 4 * c + h // GH - 1)
                        A_(pr[:, h % PBUF].rearrange("p t s -> p (t s)"), psum[S2B + h % 2][:], ACT.Exp,
                           scale=SCALE).then_inc(p_ready, 1)
                if B:
                    act.wait_ge(v_ps, d + 1)
                    if later(c, 1):
                        act.wait_ge(pv_done, 4 * c)
                    else:
                        act.wait_ge(pool_const, 5)
                    A_(va[:, 1 - b, :, :, 0:DH], psum[X][:].rearrange("p (t h r) -> p t h r", t=QT, h=NH),
                       ACT.Copy).then_inc(v_ready, 1)

            rolled(act, SPAN, step)

        @block.vector
        def _(dve):
            ch = Chain(dve, dve_chain)
            link = ch.link

            def stats(which, tile):
                for t in range(QT):
                    ch.tick(nc.vector.bn_stats(bn[:, which, t], tile(t)))

            def written():
                dve.wait_ge(dve_chain, ch.base + ch.k)

            def collect(which, done):
                for t in range(QT):
                    last = nc.vector.bn_aggr(mv[:, which, t], bn[:, which, t])
                    if t < QT - 1:
                        ch.tick(last)
                last.then_inc(done, 1)

            def ln1_stats(c):
                stats(0, lambda t: h_tok[:, c * QT + t])

            nc.vector.memset(qs[ZERO:MROW, 0].bitcast(F32), 0.0).then_inc(zeroed, 1)
            dve.wait_ge(h_first, 16)
            ln1_stats(0)
            written()
            collect(0, ln1_stat)
            nc.vector.memset(qs[ZERO:MROW, 1].bitcast(F32), 0.0).then_inc(zeroed, 1)

            def step(c, b, i):
                ln, A, B, Cc, end, fin = has(c)
                a, d, t, u = c + 2, c + 1, c - 1, c - 2

                def max_lo(n, s):
                    dve.wait_ge(m_hi, 2 * n + s + 1)
                    STT(out=mp[:, 1], in0=psum[(Y, X)[s]][0:H8, 0:S], scalar=-1.0,
                        in1=mp[:, 0].bitcast(F32), op0=ALU.mult, op1=ALU.subtract).then_inc(m_lo, 1)

                def parts_lo(which, bank, hi, lo):
                    dve.wait_ge(hi, 2 * a + 2)
                    for s in range(2):
                        STT(out=qk[:, b, which, 1, s], in0=psum[bank][:, s * S:(s + 1) * S],
                            scalar=bqk[:, 2 * which + s:2 * which + s + 1], in1=qk[:, b, which, 0, s].bitcast(F32),
                            op0=ALU.add, op1=ALU.subtract).then_inc(lo, 1)

                def normalize_o(q, bank):
                    dve.wait_ge(ot_ps, 2 * t + q + 1)
                    o_v = psum[bank][:].rearrange("p (h r) -> p h r", h=NH)
                    link(nc.vector.reciprocal(den[:], o_v[:, :, DH]))
                    TT(on[:, q].rearrange("p (h r) -> p h r", h=NH), o_v[:, :, 0:DH],
                       den[:].unsqueeze(2).to_broadcast([P, NH, DH]), ALU.mult).then_inc(on_ready, 1)

                for h in range(NH):
                    if h == 2 and A:
                        dve.wait_ge(xt_hi, a + 1)
                        TT(xt[:, b, 1].rearrange("p t s -> p (t s)"), psum[Y][:],
                           xt[:, b, 0].bitcast(F32).rearrange("p t s -> p (t s)"), ALU.subtract).then_inc(xt_lo, 1)
                    if h == 3 and Cc:
                        max_lo(c, 1)
                    if h == 5 and A:
                        parts_lo(0, X, q_hi, q_lo)
                    if h == 6 and A:
                        parts_lo(1, Y, k_hi, k_lo)
                    if h == 8 and end:
                        normalize_o(0, Y)
                    if h == 9 and end:
                        dve.wait_ge(on_ready, 2 * t + 1)
                        normalize_o(1, X)
                    if h == 11 and B:
                        max_lo(d, 0)
                    if h == 13 and end:
                        dve.wait_ge(ont_hi, t + 1)
                        TT(ot[:, 1].rearrange("p t s -> p (t s)"), psum[X][:],
                           ot[:, 0].bitcast(F32).rearrange("p t s -> p (t s)"), ALU.subtract).then_inc(ont_lo, 1)
                    if h == 14 and end:
                        dve.wait_ge(pj_ps, t + 1)
                        dve.wait_ge(hb, t + 1)
                        ht = h_tok[:, tiles(t)]
                        TT(ht, psum[Y][:].rearrange("p (t d) -> p t d", t=QT), ht, ALU.add).then_inc(h1_ready, 1)
                        dve.wait_ge(h1_ready, t + 1)
                    if (h == 15 and end) or (h == 5 and ln):
                        written()
                        if h == 15 and fin:
                            dve.wait_ge(y_ready, u + 1)
                    if B:
                        if h == 0 and later(d, 1):
                            dve.wait_ge(mt_ps, 2 * d - 1)
                        if h == H8 and later(c, 0):
                            dve.wait_ge(mt_ps, 2 * c + 2)
                        dve.wait_ge(s1_ps, 16 * d + h + 1)
                        nc.vector.tensor_reduce(mx[:, :, h], psum[SA + h % 2][:].rearrange("p (t s) -> p t s", t=QT),
                                                AX.X, ALU.max).then_inc(s1_max, 1)
                    if h == 4 and ln:
                        if isinstance(c, int):
                            for k in range(4):
                                if k == (c + 3) // 4 or c == 1:
                                    dve.wait_ge(h_loaded[k], 16)
                        ln1_stats(c + 3)
                    if h == 5 and ln:
                        collect(0, ln1_stat)
                    if h == 14 and end:
                        stats(1, lambda q: h_tok[:, t * QT + q])
                    if h == 15 and end:
                        collect(1, ln2_stat)

            rolled(dve, SPAN, step, ch)

        @block.tensor
        def _(pe):
            def product(out, pairs):
                for k, (l, r) in enumerate(pairs):
                    last = mm(out, l, r, start=(k == 0), stop=(k == len(pairs) - 1))
                return last

            PARTS = ((0, 0), (1, 0), (0, 1))

            def step(c, b, i):
                ln, A, B, Cc, end, fin = has(c)
                a, d, t, u = c + 2, c + 1, c - 1, c - 2

                def free(n, *read):
                    for done in read:
                        pe.wait_ge(done, n)

                def four(bank, src):
                    for dt in range(DT):
                        for q in range(QT):
                            last = nc.tensor.transpose(psum[bank][:, dt * S + q * P:dt * S + (q + 1) * P],
                                                       src[:, q, dt * P:(dt + 1) * P], ident[:])
                    return last

                def x_transposed():
                    pe.wait_ge(xn_ready, a + 1)
                    if later(t, 1):
                        free(t, h1_ready)
                    elif later(d, 1):
                        free(2 * d - 1, m_hi, m_lo)
                    elif later(a, 1):
                        free(2 * a, k_hi, k_lo)
                    four(Y, xn).then_inc(xt_ps, 1)

                def max_transposed(n, s):
                    pe.wait_ge(s1_max, 16 * n + 8 * s + 8)
                    if s:
                        free(n + 1, v_ready)
                    elif end:
                        free(2 * t + 1, on_ready)
                    else:
                        free(2 * a + 2, k_hi, k_lo)
                    for q in range(QT):
                        last = nc.tensor.transpose(psum[(Y, X)[s]][0:H8, q * P:(q + 1) * P],
                                                   mx[:, q, H8 * s:H8 * s + H8], ident[:])
                    last.then_inc(mt_ps, 1)

                def q_or_k(which, bank, done):
                    for s in range(2):
                        last = product(psum[bank][:, s * S:(s + 1) * S],
                                       [(wqk[:, l, dt, 2 * which + s].rearrange("p r h -> p (r h)"), xt[:, b, r, dt])
                                        for dt in range(DT) for l, r in PARTS])
                    last.then_inc(done, 1)

                def q_product():
                    if Cc:
                        free(2 * c + 2, m_hi, m_lo)
                    elif later(a, 1):
                        free(2 * a, q_hi, q_lo)
                    pe.wait_ge(xt_hi, a + 1)
                    pe.wait_ge(xt_lo, a + 1)
                    q_or_k(0, X, q_ps)

                def y_transposed():
                    pe.wait_ge(y_ready, u + 1)
                    if end:
                        free(t + 1, ont_hi, ont_lo)
                    else:
                        free(u, yt_ready)
                    four(X, y).then_inc(yt_ps, 1)

                def o_transposed(q):
                    if q:
                        if A:
                            free(2 * a + 2, q_hi, q_lo)
                        elif Cc:
                            free(2 * c + 2, m_hi, m_lo)
                        else:
                            free(u, yt_ready)
                    else:
                        pe.wait_ge(o_ready, 2 * t + 2)
                        if A:
                            free(2 * a + 2, k_hi, k_lo)
                        else:
                            free(t, h1_ready)
                    for g in range(4):
                        last = nc.tensor.transpose(psum[(Y, X)[q]][:, g * P:(g + 1) * P],
                                                   o_sb[:, g, q * P:(q + 1) * P], ident[:])
                    last.then_inc(ot_ps, 1)

                def projection():
                    if B:
                        free(2 * d + 1, m_hi, m_lo)
                    pe.wait_ge(ont_hi, t + 1)
                    pe.wait_ge(ont_lo, t + 1)
                    for q in range(QT):
                        last = product(psum[Y][:, q * D:(q + 1) * D],
                                       [(ot[:, l, dt, q * P:(q + 1) * P], wo[:, r, dt])
                                        for dt in range(DT) for l, r in PARTS])
                    last.then_inc(pj_ps, 1)

                def v_product():
                    if fin:
                        free(u + 1, yt_ready)
                    elif end:
                        free(t + 1, ont_hi, ont_lo)
                    else:
                        free(2 * a + 2, q_hi, q_lo)
                    for q in range(QT):
                        last = product(psum[X][:, q * D:(q + 1) * D],
                                       [(xt[:, 1 - b, l, dt, q * P:(q + 1) * P], wv[:, r, dt])
                                        for dt in range(DT) for l, r in PARTS])
                    last.then_inc(v_ps, 1)

                def pv(n, g, buf):
                    pe.wait_ge(p_ready, 16 * n + GH * g + GH)
                    if g == 0:
                        pe.wait_ge(v_ready, n + 1)
                    if g % 2 == 0 and later(n, 1):
                        pe.wait_ge(o_ready, 2 * n - 1 + g // 2)
                    for kt in range(QT):
                        for j in range(GH):
                            h = GH * g + j
                            last = mm(psum[POB + g // 2][32 * j:32 * j + 32, (g % 2) * S:(g % 2 + 1) * S],
                                      va[:, buf, kt, h], pr[:, h % PBUF, kt], start=(kt == 0), stop=(kt == QT - 1),
                                      tile_position=(0, 32 * j))
                    last.then_inc(pv_done, 1)

                for h in range(NH):
                    if isinstance(c, int) and c == -1 and h == 0:
                        pe.wait_ge(zeroed, 3)
                        pe.wait_ge(pool_const, 5)
                    if B:
                        if h % H8 == 0:
                            pe.wait_ge(stk[1 - b][h // H8], 128 * (i + b + 1))
                        if h >= 2 or later(d, 1):
                            pe.wait_ge(s1_max, 16 * d + h - 1)
                        for q in range(QT):
                            last = mm(psum[SA + h % 2][:, q * S:(q + 1) * S], qs[0:MROW, 1 - b, h, q * P:(q + 1) * P],
                                      ks[0:MROW, 1 - b, h], start=True, stop=True)
                        last.then_inc(s1_ps, 1)
                    if Cc:
                        if h % H8 == 0:
                            pe.wait_ge(mrow[b][h // H8], 32 * (i + 1))
                        if h >= 2 or later(c, 1):
                            pe.wait_ge(p_ready, 16 * c + h - 1)
                        for kt in range(QT):
                            last = mm(psum[S2B + h % 2][:, kt * S:(kt + 1) * S], ks[0:KROWS, b, h, kt * P:(kt + 1) * P],
                                      qs[0:KROWS, b, h], start=True, stop=True)
                        last.then_inc(s2_ps, 1)
                        if h in (5, 9, 13):
                            pv(c, (h - 5) // 4, b)
                    if h == 0 and A:
                        x_transposed()
                    if h == 1 and end:
                        pv(t, 3, 1 - b)
                    if h == 1 and Cc:
                        max_transposed(c, 1)
                    if h == 3 and A:
                        q_product()
                    if h == 4 and A:
                        q_or_k(1, Y, k_ps)
                    if h == 7 and end:
                        o_transposed(0)
                    if h == 8 and end:
                        o_transposed(1)
                    if h == 9 and B:
                        max_transposed(d, 0)
                    if h == 11 and end:
                        pe.wait_ge(on_ready, 2 * t + 2)
                        four(X, on).then_inc(ont_ps, 1)
                    if h == 13 and end:
                        projection()
                    if h == 13 and fin:
                        y_transposed()
                    if h == 14 and B:
                        v_product()

            rolled(pe, SPAN, step)


class ExpertWeights:

    def __init__(self, ctx, nc, W):
        self.w_gate, self.w_up, self.w_down, self.sw_gate, self.sw_up, self.sw_down = W
        E, D, F = self.w_gate.shape
        self.E, self.DT, self.FT = E, D // P, -(-F // P)
        self.rest = F - (self.FT - 1) * P
        self.gu_cols = self.DT * 2 * F
        self.raw = ctx.enter_context(nc.sbuf_tensor("raw", [P, 2, self.gu_cols + self.FT * D], F32))

    def views(self, b):
        return (self.raw[:, b, 0:self.gu_cols].rearrange("p (t g f) -> p t g f", t=self.DT, g=2),
                self.raw[:, b, self.gu_cols:].rearrange("p (t d) -> p t d", t=self.FT))

    def load(self, sp, n, b, done):
        shared = isinstance(n, int) and n == self.E
        wg, wu, wd = (self.sw_gate, self.sw_up, self.sw_down) if shared else (self.w_gate[n], self.w_up[n],
                                                                             self.w_down[n])
        gu, dn = self.views(b)
        full = (self.FT - 1) * P
        for k, w in ((0, wg), (1, wu)):
            sp.dma_start(gu[:, :, k], w.rearrange("(t p) f -> p t f", p=P)).then_inc(done, 16)
        sp.dma_start(dn[:, 0:self.FT - 1], wd[0:full].rearrange("(t p) d -> p t d", p=P)).then_inc(done, 16)
        sp.dma_start(dn[0:self.rest, self.FT - 1], wd[full:]).then_inc(done, 16)

    def pieces(self, b, gu, dn):
        rgu, rdn = self.views(b)
        r, f = self.rest, self.FT - 1
        return [(rgu, gu[:, 0], gu[:, 1]), (rdn[:, 0:f], dn[:, 0, 0:f], dn[:, 1, 0:f]),
                (rdn[0:r, f], dn[0:r, 0, f], dn[0:r, 1, f])]





def route(nc, router_w, router_b, ident, psum, y_t, slots, slot_of, gate, weights, CAP):
    D, E = router_w.shape
    DT = D // P
    T = y_t.shape[2] // P
    NCH = T // 4
    NS = CAP // P
    NCOL = E * NS
    LG, CUM, TOT, LIST = (4, 5), 5, 6, 7
    LISTS = [(k, half) for k in range(2) for half in range(2)]
    HALVES = [slice(0, T // 2), slice(T // 2, T)]
    V = nc.vector
    TT, TS, STT, RED = V.tensor_tensor, V.tensor_scalar, V.scalar_tensor_tensor, V.tensor_reduce

    with ExitStack() as ctx:
        def sb(name, shape, dt=F32):
            return ctx.enter_context(nc.sbuf_tensor(name, shape, dt))

        def sem(name):
            return ctx.enter_context(nc.semaphore(name))

        rw = sb("rw", [P, DT, E])
        rb = sb("rb", [E, 1])
        lg_t = sb("lg_t", [E, T * P])
        em = sb("em", [P, T, E])
        em_i = sb("em_i", [P, T, E], I32)
        prob = sb("prob", [P, T, E])
        ex = sb("ex", [P, T, E])
        hot = sb("hot", [P, 2, T, E])
        both = sb("both", [P, T, E], F32R)
        work = sb("work", [P, T, E])
        rest = sb("rest", [P, T, E])
        pos = sb("pos", [P, T, E])
        tot = sb("tot", [P, E, T])
        run = sb("run", [P, E, T])
        keep = sb("keep", [P, E, T])
        best = sb("best", [P, 2, T])
        idx = sb("idx", [P, 2, T])
        place = sb("place", [P, 2, T])
        fits = sb("fits", [P, 2, T])
        s_a = sb("s_a", [P, T])
        s_b = sb("s_b", [P, T])
        slot_f = sb("slot_f", [P, 2, T])
        slot_g = sb("slot_g", [P, 2, T])
        part = sb("part", [P, 2, T])
        col = sb("col", [P, 2, T])
        over = sb("over", [P, 2, T])
        count_i = sb("count_i", [P, P], I32)
        count = sb("count", [P, P])
        token_i = sb("token_i", [P, T], I32)
        token = sb("token", [P, T])
        hot_p = sb("hot_p", [P, 2, T, P], F32R)
        hot_col = sb("hot_col", [P, 2, T, NCOL])
        tok_col = sb("tok_col", [P, 2, T, NCOL], F32R)
        before = sb("before", [P, P])
        ones = sb("ones", [P, P])
        before_r = sb("before_r", [P, P], F32R)
        ones_r = sb("ones_r", [P, P], F32R)

        loaded, first_w = sem("r_loaded"), sem("first_w")
        col_ready, tok_ready = sem("col_ready"), sem("tok_ready")
        part_ready, list_ps = sem("part_ready"), sem("list_ps")
        const_r = sem("const_r")
        lt_ps, lt_ready, lg_ps = sem("lt_ps"), sem("lt_ready"), sem("lg_ps")
        shifted, exp_done = sem("shifted"), sem("exp_done")
        hot_ready, cum_ps, chain = sem("hot_ready"), sem("cum_ps"), sem("r_chain")

        block = ctx.enter_context(nc.Block())

        @block.sync
        def _(sp):
            sp.dma_start(rw[:], router_w.rearrange("(t p) e -> p t e", p=P)).then_inc(loaded, 16)
            sp.dma_start(rb[:], router_b.rearrange("(e o) -> e o", o=1)).then_inc(loaded, 16)
            for b in range(2):
                weights.load(sp, b, b, first_w)
            sp.wait_ge(first_w, 128)

        @block.gpsimd
        def _(pool):
            G = nc.gpsimd
            G.memset(ones[:], 1.0).then_inc(const_r, 1)
            pool.wait_ge(const_r, 1)
            G.affine_select(out=before[:], in_=ones[:], compare_op=ALU.is_ge, fill=0.0, base=-1,
                            pattern=[[1, P]], channel_multiplier=-1).then_inc(const_r, 1)
            G.iota(em_i[:], pattern=[[0, T], [1, E]], base=-E, channel_multiplier=0).then_inc(const_r, 1)
            G.iota(count_i[:], pattern=[[1, P]], base=0, channel_multiplier=0).then_inc(const_r, 1)
            G.iota(token_i[:], pattern=[[P, T]], base=0, channel_multiplier=1).then_inc(const_r, 1)
            G.memset(keep[:], 1.0).then_inc(const_r, 1)
            pool.wait_ge(const_r, 6)
            G.memset(keep[:, :, 0:1], 0.0).then_inc(const_r, 1)
            for k, half in LISTS:
                h = HALVES[half]
                pool.wait_ge(col_ready, 2 * k + half + 1)
                G.tensor_tensor(tok_col[:, k, h], hot_col[:, k, h],
                                token[:, h].unsqueeze(2).to_broadcast([P, T // 2, NCOL]), ALU.mult).then_inc(tok_ready, 1)

        @block.scalar
        def _(act):
            act.wait_ge(loaded, 32)
            for n in range(NCH):
                act.wait_ge(lt_ps, n + 1)
                nc.scalar.activation(lg_t[:, n * 512:(n + 1) * 512], psum[n % 4][0:E, :], ACT.Identity,
                                     bias=rb[:, 0:1]).then_inc(lt_ready, 1)
                if n in (NCH // 2 + 1, NCH - 1):
                    g = n // (NCH - 1)
                    act.wait_ge(shifted, g + 1)
                    nc.scalar.activation(ex[:, HALVES[g]], work[:, HALVES[g]], ACT.Exp).then_inc(exp_done, 1)

        @block.tensor
        def _(pe):
            pe.wait_ge(loaded, 32)
            def token_major(g):
                for n in range(g * NCH // 2, (g + 1) * NCH // 2):
                    pe.wait_ge(lt_ready, n + 1)
                    for k in range(4):
                        t = 4 * n + k
                        at = (t % (T // 2)) * E
                        last = nc.tensor.transpose(psum[LG[g]][:, at:at + E], lg_t[:, t * P:(t + 1) * P],
                                                   ident[0:E, 0:E])
                last.then_inc(lg_ps, 1)

            for n in range(NCH):
                if n >= 4:
                    pe.wait_ge(lt_ready, n - 3)
                for dt in range(DT):
                    last = nc.tensor.matmul(psum[n % 4][0:E, :], rw[:, dt], y_t[:, dt, n * 512:(n + 1) * 512],
                                            start=(dt == 0), stop=(dt == DT - 1))
                last.then_inc(lt_ps, 1)
                if n == NCH // 2:
                    token_major(0)
            token_major(1)
            pe.wait_ge(hot_ready, 1)
            flat = both[:].rearrange("p t e -> p (t e)")
            nc.tensor.matmul(psum[CUM][:], before_r[:], flat, start=True, stop=True)
            nc.tensor.matmul(psum[TOT][:], ones_r[:], flat, start=True, stop=True).then_inc(cum_ps, 1)
            for k, half in LISTS:
                pe.wait_ge(part_ready, 2 * k + half + 1)
                pe.wait_ge(tok_ready, 2 * k + half + 1)
                for t in range(T)[HALVES[half]]:
                    last = nc.tensor.matmul(psum[LIST][:, 0:NCOL], hot_p[:, k, t], tok_col[:, k, t],
                                            start=(k == 0 and t == 0), stop=(k == 1 and t == T - 1))
            last.then_inc(list_ps, 1)

        @block.vector
        def _(dve):
            ch = Chain(dve, chain)
            link = ch.link
            te = lambda b: psum[b][:].rearrange("p (t e) -> p t e", t=T)
            dve.wait_ge(const_r, 7)
            ch.tick(V.tensor_copy(em[:], em_i[:]))
            ch.tick(V.tensor_copy(count[:], count_i[:]))
            ch.tick(V.tensor_copy(token[:], token_i[:]))
            ch.tick(V.tensor_copy(before_r[:], before[:]))
            ch.tick(V.tensor_copy(ones_r[:], ones[:]))
            for g, h in enumerate(HALVES):
                shape = [P, T // 2, E]
                logits = psum[LG[g]][:, 0:T // 2 * E].rearrange("p (t e) -> p t e", e=E)
                wide = lambda x: x.unsqueeze(2).to_broadcast(shape)
                w = work[:, h]
                dve.wait_ge(lg_ps, g + 1)
                link(RED(s_a[:, h], logits, AX.X, ALU.max))
                TT(w, logits, wide(s_a[:, h]), ALU.subtract).then_inc(shifted, 1)
                dve.wait_ge(exp_done, g + 1)
                link(RED(s_b[:, h], ex[:, h], AX.X, ALU.add))
                link(V.reciprocal(s_a[:, h], s_b[:, h]))
                link(TT(prob[:, h], ex[:, h], wide(s_a[:, h]), ALU.mult))
                for k, src in ((0, prob), (1, rest)):
                    link(RED(best[:, k, h], src[:, h], AX.X, ALU.max))
                    link(TT(w, src[:, h], wide(best[:, k, h]), ALU.is_equal))
                    link(TT(w, w, em[:, h], ALU.mult))
                    link(RED(idx[:, k, h], w, AX.X, ALU.min))
                    link(TT(hot[:, k, h], em[:, h], wide(idx[:, k, h]), ALU.is_equal))
                    if k == 0:
                        link(STT(out=rest[:, h], in0=hot[:, 0, h], scalar=-4.0, in1=prob[:, h], op0=ALU.mult,
                                 op1=ALU.add))
            TT(both[:], hot[:, 0], hot[:, 1], ALU.add).then_inc(hot_ready, 1)
            link(TT(s_a[:], best[:, 0], best[:, 1], ALU.add))
            link(TS(s_a[:], s_a[:], 1e-9, None, ALU.add))
            link(V.reciprocal(s_b[:], s_a[:]))
            dve.wait_ge(cum_ps, 1)
            link(V.tensor_copy(tot[:], psum[TOT][:].rearrange("p (t e) -> p e t", t=T)))
            link(V.tensor_tensor_scan(run[:].rearrange("p e t -> p (e t)"), keep[:].rearrange("p e t -> p (e t)"),
                                      tot[:].rearrange("p e t -> p (e t)"), 0.0, ALU.mult, ALU.add))
            link(TT(run[:], run[:], tot[:], ALU.subtract))
            link(TT(pos[:], te(CUM), run[:].rearrange("p e t -> p t e"), ALU.add))
            for k in range(2):
                link(TT(work[:], hot[:, k], pos[:], ALU.mult))
                link(RED(place[:, k], work[:], AX.X, ALU.add))
            link(TS(fits[:], place[:], float(CAP), None, ALU.is_lt))
            link(TS(over[:], place[:], float(P), None, ALU.is_ge))
            for m in range(2, NS):
                link(STT(out=over[:], in0=place[:], scalar=float(P * m), in1=over[:], op0=ALU.is_ge, op1=ALU.add))
            ch.tick(STT(out=part[:], in0=over[:], scalar=float(-P), in1=place[:], op0=ALU.mult, op1=ALU.add))
            ch.tick(STT(out=col[:], in0=idx[:], scalar=float(NS), in1=over[:], op0=ALU.mult, op1=ALU.add))
            ch.tick(TS(slot_f[:], fits[:], float(-NCOL), float(2 * NCOL), ALU.mult, ALU.add))
            link(TS(slot_g[:], place[:], float(CAP - 1), float(E * CAP), ALU.min, ALU.add))
            link(TT(col[:], col[:], slot_f[:], ALU.add))
            for k, half in LISTS:
                h = HALVES[half]
                shape = [P, T // 2, NCOL]
                TT(hot_col[:, k, h], count[:, 0:NCOL].unsqueeze(1).to_broadcast(shape),
                   col[:, k, h].unsqueeze(2).to_broadcast(shape), ALU.is_equal).then_inc(col_ready, 1)
                shape = [P, T // 2, P]
                TT(hot_p[:, k, h], count[:].unsqueeze(1).to_broadcast(shape),
                   part[:, k, h].unsqueeze(2).to_broadcast(shape), ALU.is_equal).then_inc(part_ready, 1)
            link(STT(out=slot_f[:], in0=idx[:], scalar=float(CAP), in1=slot_g[:], op0=ALU.mult, op1=ALU.add))
            V.tensor_copy(slot_of[:], slot_f[:])
            link(TT(gate[:], best[:], fits[:], ALU.mult))
            TT(gate[:], gate[:], s_b[:].unsqueeze(1).to_broadcast([P, 2, T]), ALU.mult)
            dve.wait_ge(list_ps, 1)
            V.tensor_copy(slots[:].rearrange("p e s -> p (e s)"), psum[LIST][:, 0:NCOL])


def experts(nc, weights, ident, psum, h_tok, y_t, y_dram, slots, slot_of, gate, e_dram, out, CAP):
    E, D, F = weights.w_gate.shape
    DT = D // P
    FT = -(-F // P)
    FW = [min(P, F - P * f) for f in range(FT)]
    T = y_t.shape[2] // P
    NS = CAP // P
    XB0, GB, UB, DB = 0, 2, 4, 6
    V, A_, G = nc.vector, nc.scalar.activation, nc.gpsimd
    TT, STT = V.tensor_tensor, V.scalar_tensor_tensor
    mm = nc.tensor.matmul
    PARTS = ((0, 0), (1, 0), (0, 1))
    NU = T // 4
    YG = 8

    with ExitStack() as ctx:
        def sb(name, shape, dt=F32):
            return ctx.enter_context(nc.sbuf_tensor(name, shape, dt))

        sgu = sb("sgu", [P, 2, DT, 2, F], F32R)
        sdn = sb("sdn", [P, 2, FT, D], F32R)
        egu = sb("egu", [P, 2, 2, DT, 2, F], F32R)
        edn = sb("edn", [P, 2, 2, FT, D], F32R)
        xt = sb("xt4", [P, 2, 2, DT * CAP], F32R)
        hid = sb("hid", [P, 2, 2, FT, CAP], F32R)
        sg = sb("sg", [P, 2, 512])
        hf = sb("hf", [P, 2, 512])
        xg = sb("xg", [P, 2, NS, D])
        yb = sb("yb", [P, NS, D])
        yg = weights.raw[:].rearrange("p b n -> p (b n)")[:, 0:YG * 2 * D].rearrange("p (k m d) -> p k m d", k=YG, m=2)

        def phase(name, shared, n_units, span, more_sems, sp_more, pool_more, dve_more):
            with ExitStack() as pctx:
                def sem(s):
                    return pctx.enter_context(nc.semaphore(f"{s}_{name}"))

                NT = 4 if shared else NS
                N = NT * P
                COLS = [(0, N)] if shared else [(0, N // 2), (N // 2, N // 2)]
                K = FT * len(COLS)
                R = (NT + 1) // 2
                XB = -(-DT * NS * P // 512)
                x_ps, x_hi, x_lo = sem("x_ps"), sem("x_hi"), sem("x_lo")
                gu_ps, sg_ready, hf_ready = sem("gu_ps"), sem("sg_ready"), sem("hf_ready")
                hh_ready, hl_ready = sem("hh_ready"), sem("hl_ready")
                d_ps, d_done = sem("d_ps"), sem("d_done")
                w_hi, w_lo = sem("w_hi"), sem("w_lo")
                w_in, g_in, y_out = [None] * 3 if shared else [[sem(f"{s}{b}") for b in range(2)]
                                                       for s in ("w_in", "g_in", "y_out")]
                extra = {k: sem(k) for k in more_sems}
                NX = 1 if shared else XB
                ahead = 1 if shared else 0
                x_next = sem("x_next")

                TURN = {} if shared else {K - 4 + j: j for j in range(XB)}
                TAKE = {1: 0} if shared else {K - 3 + j: j for j in range(XB)}

                def target(n, b):
                    return (sgu, sdn) if isinstance(n, int) and n == E else (egu[:, b], edn[:, b])

                def has(n):
                    if not isinstance(n, int):
                        return True, True, True
                    return n < n_units, n + 1 < n_units, n >= 1

                def later(n, k):
                    return not isinstance(n, int) or n >= k

                def gu_w(b, part, dt, k, f):
                    w = sgu[:, part] if shared else egu[:, b, part]
                    return w[:, dt, k, f * P:f * P + FW[f]]

                def dn_w(b, part, f):
                    w = sdn[:, part] if shared else edn[:, b, part]
                    return w[0:FW[f], f]

                def x_view(b, part):
                    return xt[:, b, part, 0:DT * N].rearrange("p (t s) -> p t s", t=DT)

                first_x = [xt[:, 0, part, 0:DT * 4 * P].rearrange("p (t s) -> p t s", t=DT) for part in range(2)]

                block = pctx.enter_context(nc.Block())

                @block.tensor
                def _(pe):
                    def gate_up(n, b, i):
                        if not shared:
                            pe.wait_ge(w_lo, 3 * n + 1)
                            pe.wait_ge(w_hi, 3 * n + 1)
                        if not shared or later(n, 1):
                            pe.wait_ge(x_hi, NX * (n + 1 - ahead))
                            pe.wait_ge(x_lo, NX * (n + 1 - ahead))
                        for c, (c0, cw) in enumerate(COLS):
                            for f in range(FT):
                                j = c * FT + f
                                q = K * n + j
                                k = (K * b + j) % 2
                                if later(n, 1) or j >= 2:
                                    pe.wait_ge(hf_ready, q - 1)
                                for g, bank in ((0, GB), (1, UB)):
                                    m = 0
                                    for dt in range(DT):
                                        for l, r in PARTS:
                                            last = mm(psum[bank + k][0:FW[f], 0:cw], gu_w(b, l, dt, g, f),
                                                      x_view(b, r)[:, dt, c0:c0 + cw], start=(m == 0),
                                                      stop=(m == 3 * DT - 1))
                                            m += 1
                                last.then_inc(gu_ps, 1)
                                if j in TURN and has(n)[1]:
                                    turn(n + 1, 1 - b, i + b, TURN[j])

                    def turn(n, b, i, j):
                        if j == 0:
                            pe.wait_ge(g_in[b], 16 * NS * (i + 1))
                        k = (XB * b + j) % 2
                        if later(n, 1) or j >= 2:
                            pe.wait_ge(x_lo, XB * n + j - 1)
                        for m in range(4 * j, min(4 * j + 4, DT * NS)):
                            dt, s = divmod(m, NS)
                            last = nc.tensor.transpose(psum[XB0 + k][:, (m % 4) * P:(m % 4 + 1) * P],
                                                       xg[:, b, s, dt * P:(dt + 1) * P], ident[:])
                        last.then_inc(x_ps, 1)

                    def down(n, b):
                        pe.wait_ge(hh_ready, K * n + K)
                        pe.wait_ge(hl_ready, K * n + K)
                        if not shared:
                            pe.wait_ge(w_lo, 3 * n + 3)
                            pe.wait_ge(w_hi, 3 * n + 3)
                        for j in range(R):
                            k = (R * b + j) % 2
                            if later(n, 1) or j >= 2:
                                pe.wait_ge(d_done, R * n + j - 1)
                            for s in range(2 * j, min(2 * j + 2, NT)):
                                m = 0
                                for f in range(FT):
                                    for l, r in PARTS:
                                        last = mm(psum[DB + k][:, (s % 2) * D:(s % 2 + 1) * D],
                                                  hid[0:FW[f], b, l, f, s * P:(s + 1) * P], dn_w(b, r, f),
                                                  start=(m == 0), stop=(m == 3 * FT - 1))
                                        m += 1
                            last.then_inc(d_ps, 1)

                    for j in TURN.values():
                        turn(0, 0, 0, j)

                    def step(n, b, i):
                        this, following, before = has(n)
                        if this:
                            gate_up(n, b, i)
                        if before:
                            down(n - 1, 1 - b)

                    rolled(pe, span, step)

                @block.scalar
                def _(act):
                    def take_x(n, b, j):
                        if j == 0 and later(n, 2):
                            act.wait_ge(gu_ps, K * n - K)
                        if shared:
                            t0 = NT * n * P
                            A_(x_view(b, 0), y_t[:, :, t0:t0 + N], ACT.Copy).then_inc(x_hi, 1)
                        else:
                            act.wait_ge(x_ps, XB * n + j + 1)
                            w = min(512, DT * N - 512 * j)
                            A_(xt[:, b, 0, 512 * j:512 * j + w], psum[XB0 + (XB * b + j) % 2][:, 0:w],
                               ACT.Copy).then_inc(x_hi, 1)

                    def hi(n, b, j):
                        c0, cw = COLS[j // FT]
                        f = j % FT
                        k = (K * b + j) % 2
                        act.wait_ge(hf_ready, K * n + j + 1)
                        if j == 0 and later(n, 2):
                            act.wait_ge(d_ps, R * n - R)
                        A_(hid[0:FW[f], b, 0, f, c0:c0 + cw], hf[0:FW[f], k, 0:cw], ACT.Copy).then_inc(hh_ready, 1)

                    def step(n, b, i):
                        this, following, before = has(n)
                        for j in range(K if this else 0):
                            f = j % FT
                            cw = COLS[j // FT][1]
                            k = (K * b + j) % 2
                            act.wait_ge(gu_ps, K * n + j + 1)
                            if later(n, 1) or j >= 2:
                                act.wait_ge(hf_ready, K * n + j - 1)
                            A_(sg[0:FW[f], k, 0:cw], psum[GB + k][0:FW[f], 0:cw], ACT.Silu).then_inc(sg_ready, 1)
                            if j:
                                hi(n, b, j - 1)
                            if j in TAKE and following:
                                take_x(n + 1, 1 - b, TAKE[j])
                        if this:
                            hi(n, b, K - 1)
                        if not shared and not this:
                            A_(first_x[0], y_t[:, :, 0:4 * P], ACT.Copy).then_inc(x_next, 1)
                        if before and not shared:
                            m = n - 1
                            for j in range(R):
                                act.wait_ge(d_ps, R * m + j + 1)
                                if j == 0 and later(m, 1):
                                    act.wait_ge(y_out[b], 16 * i)
                                w = min(2, NT - 2 * j)
                                A_(yb[:, 2 * j:2 * j + w].rearrange("p s d -> p (s d)"),
                                   psum[DB + (R * (1 - b) + j) % 2][:, 0:w * D], ACT.Copy).then_inc(d_done, 1)

                    if not shared:
                        for j in TAKE.values():
                            take_x(0, 0, j)
                    rolled(act, span, step)

                @block.vector
                def _(dve):
                    def take_x(n, b, j):
                        if shared:
                            t0 = NT * n * P
                            dve.wait_ge(x_hi, n)
                            TT(x_view(b, 1), y_t[:, :, t0:t0 + N], x_view(b, 0).bitcast(F32),
                               ALU.subtract).then_inc(x_lo, 1)
                        else:
                            dve.wait_ge(x_hi, XB * n + j + 1)
                            w = min(512, DT * N - 512 * j)
                            TT(xt[:, b, 1, 512 * j:512 * j + w], psum[XB0 + (XB * b + j) % 2][:, 0:w],
                               xt[:, b, 0, 512 * j:512 * j + w].bitcast(F32), ALU.subtract).then_inc(x_lo, 1)

                    def split_gate_up(n, b, i):
                        if later(n, 2):
                            dve.wait_ge(w_in[b], 64 * i)
                            dve.wait_ge(gu_ps, K * n - K)
                        whole, high, _ = weights.pieces(b, *target(n, b))[0]
                        V.tensor_copy(high, whole).then_inc(w_hi, 1)

                    def split_down(n, b):
                        if later(n, 2):
                            dve.wait_ge(d_ps, R * n - R)
                        for whole, high, _ in weights.pieces(b, *target(n, b))[1:]:
                            V.tensor_copy(high, whole).then_inc(w_hi, 1)

                    def lo(n, b, j):
                        c0, cw = COLS[j // FT]
                        f = j % FT
                        k = (K * b + j) % 2
                        dve.wait_ge(hh_ready, K * n + j + 1)
                        TT(hid[0:FW[f], b, 1, f, c0:c0 + cw], hf[0:FW[f], k, 0:cw],
                           hid[0:FW[f], b, 0, f, c0:c0 + cw].bitcast(F32), ALU.subtract).then_inc(hl_ready, 1)

                    def step(n, b, i):
                        this, following, before = has(n)
                        for j in range(K if this else 0):
                            f = j % FT
                            cw = COLS[j // FT][1]
                            k = (K * b + j) % 2
                            dve.wait_ge(sg_ready, K * n + j + 1)
                            if later(n, 1) or j >= 2:
                                dve.wait_ge(hl_ready, K * n + j - 1)
                            TT(hf[0:FW[f], k, 0:cw], psum[UB + k][0:FW[f], 0:cw], sg[0:FW[f], k, 0:cw],
                               ALU.mult).then_inc(hf_ready, 1)
                            if j:
                                lo(n, b, j - 1)
                            if j in TAKE and following:
                                take_x(n + 1, 1 - b, TAKE[j])
                            if j == 1 and not shared:
                                split_gate_up(n + 1, 1 - b, i + b)
                            if shared and before:
                                for q in range(NT * j // K, NT * (j + 1) // K):
                                    dve_more(dve, extra, NT * (n - 1) + q)
                        if this:
                            lo(n, b, K - 1)
                        if this and not shared:
                            split_down(n + 1, 1 - b)
                        if not shared and not this:
                            dve.wait_ge(x_next, 1)
                            TT(first_x[1], y_t[:, :, 0:4 * P], first_x[0].bitcast(F32), ALU.subtract)
                        if before and shared:
                            m = n - 1
                            if not this:
                                for q in range(NT):
                                    dve_more(dve, extra, NT * m + q)
                            for j in range(R):
                                dve.wait_ge(d_ps, R * m + j + 1)
                                ht = h_tok[:, bass.ds(NT * m + 2 * j, 2)]
                                TT(ht, psum[DB + (R * (1 - b) + j) % 2][:].rearrange("p (t d) -> p t d", t=2), ht,
                                   ALU.add).then_inc(d_done, 1)

                    if not shared:
                        split_gate_up(0, 0, 0)
                        whole, high, low = weights.pieces(0, *target(0, 0))[0]
                        dve.wait_ge(w_hi, 1)
                        TT(low, whole, high.bitcast(F32), ALU.subtract).then_inc(w_lo, 1)
                        split_down(0, 0)
                    if not shared:
                        for j in TAKE.values():
                            take_x(0, 0, j)
                    rolled(dve, span, step, None)

                @block.gpsimd
                def _(pool):
                    if not shared:
                        def split_lo(n, b, first, end):
                            pieces = weights.pieces(b, *target(n, b))
                            for k, (whole, high, low) in list(enumerate(pieces))[first:end]:
                                pool.wait_ge(w_hi, 3 * n + k + 1)
                                G.tensor_tensor(low, whole, high.bitcast(F32), ALU.subtract).then_inc(w_lo, 1)

                        def fetch(n, b):
                            if n >= 2:
                                pool.wait_ge(x_ps, XB * (n - 1))
                            for s in range(NS):
                                G.indirect_dma_start(xg[:, b, s], None, y_dram,
                                                     bass.IndirectOffsetOnAxis(ap=slots[:, n, s:s + 1], axis=0)
                                                     ).then_inc(g_in[b], 16)

                        fetch(0, 0)
                        for n in range(n_units + 1):
                            if n:
                                split_lo(n, n % 2, 0, 1)
                            if n + 1 < n_units:
                                fetch(n + 1, (n + 1) % 2)
                            if n == 0:
                                pool.wait_ge(w_lo, 1)
                            split_lo(n, n % 2, 1, 3)
                    pool_more(pool, extra)

                @block.sync
                def _(sp):
                    if not shared:
                        e_v = e_dram.rearrange("(e s p) d -> e p s d", e=E, p=P)

                        def step(n, b, i):
                            if not isinstance(n, int) or n + 2 <= n_units:
                                sp.wait_ge(w_lo, 3 * n + 3)
                                weights.load(sp, n + 2, b, w_in[b])
                            if later(n, 1):
                                sp.wait_ge(d_done, R * n)
                                sp.dma_start(e_v[n - 1], yb[:]).then_inc(y_out[1 - b], 16)

                        rolled(sp, span, step)
                        for b in range(2):
                            sp.wait_ge(y_out[b], 16 * n_units // 2)
                    sp_more(sp, extra, d_done)

        none = lambda *a: None

        phase("ex", False, E, (0, 2, E - 2, E + 1), (), none, none, none)

        order = [(t, t % YG) for t in range(T)]

        def gather(pool, s):
            for t, k in order:
                if t >= YG:
                    pool.wait_ge(s["comb"], 2 * (t - YG) + 2)
                for m in range(2):
                    G.indirect_dma_start(yg[:, k, m], None, e_dram,
                                         bass.IndirectOffsetOnAxis(ap=slot_of[:, m, t:t + 1], axis=0)
                                         ).then_inc(s[f"yg{k}"], 16)

        def combine(dve, s, t):
            k = t % YG
            dve.wait_ge(s[f"yg{k}"], 32 * (t // YG + 1))
            ht = h_tok[:, t]
            for m in range(2):
                STT(out=ht, in0=yg[:, k, m], scalar=gate[:, m, t:t + 1], in1=ht, op0=ALU.mult,
                    op1=ALU.add).then_inc(s["comb"], 1)
                dve.wait_ge(s["comb"], 2 * t + m + 1)

        def store(sp, s, d_done):
            o_v = out.rearrange("c (t p) d -> p (c t) d", p=P)
            for g in range(T // 4):
                sp.wait_ge(s["comb"], 8 * g + 8)
                sp.wait_ge(d_done, 2 * g + 2)
                sp.dma_start(o_v[:, 4 * g:4 * g + 4], h_tok[:, 4 * g:4 * g + 4]).then_inc(s["out_st"], 16)
            sp.wait_ge(s["out_st"], 16 * (T // 4))

        phase("sb", True, NU, (0, NU, NU, NU + 1), [f"yg{k}" for k in range(YG)] + ["comb", "out_st"],
              store, gather, combine)


def vision_tower_block(nc, x, log_dt, inv_A_real, A_imag, B_ri, W_qkv, b_qkv, W_out, b_out, router_w, router_b,
                       w_gate, w_up, w_down, sw_gate, sw_up, sw_down, out):
    C, S, D = out.shape
    E = router_w.shape[1]
    TOPK = 2
    TILES = C * S // P
    CAP = -(-5 * C * S * TOPK // (4 * E))

    h_dram = nc.dram_tensor("h_scratch", [C, S, D], F32).ap()
    y_dram = nc.dram_tensor("y_scratch", [C * S, D], F32).ap()
    e_dram = nc.dram_tensor("expert_rows_scratch", [E * CAP, D], F32).ap()

    with ExitStack() as ctx:
        def sb(name, shape, dt=F32):
            return ctx.enter_context(nc.sbuf_tensor(name, shape, dt))

        psum = [ctx.enter_context(nc.psum_tensor(f"bank{i}", [P, 512], F32)) for i in range(8)]
        ident = sb("ident", [P, P])
        with ExitStack() as attention:
            attn = AttentionWeights(attention, nc, W_qkv, b_qkv, W_out, b_out)
            make_tokens(nc, x, log_dt, inv_A_real, A_imag, B_ri, ident, psum, h_dram, attn)
            h_tok = ctx.enter_context(nc.sbuf_tensor("h_tok", [P, TILES, D], F32, side="right"))
            y_t = ctx.enter_context(nc.sbuf_tensor("y_t", [P, D // P, C * S], F32, side="right"))
            attend(nc, h_dram, attn, ident, psum, h_tok, y_t, y_dram)
        slots = sb("slots", [P, E, CAP // P], U32)
        slot_of = sb("slot_of", [P, TOPK, TILES], U32)
        gate = sb("gate", [P, TOPK, TILES])
        weights = ExpertWeights(ctx, nc, (w_gate, w_up, w_down, sw_gate, sw_up, sw_down))
        route(nc, router_w, router_b, ident, psum, y_t, slots, slot_of, gate, weights, CAP)
        experts(nc, weights, ident, psum, h_tok, y_t, y_dram, slots, slot_of, gate, e_dram, out, CAP)


_INS = ['x', 'L0_tok_log_dt', 'L0_tok_inv_A_real', 'L0_tok_A_imag', 'L0_tok_B_ri', 'L0_attn_W_qkv', 'L0_attn_b_qkv',
        'L0_attn_W_out', 'L0_attn_b_out', 'L0_ffn_router_w', 'L0_ffn_router_b', 'L0_ffn_w_gate', 'L0_ffn_w_up',
        'L0_ffn_w_down', 'L0_ffn_sw_gate', 'L0_ffn_sw_up', 'L0_ffn_sw_down']
_OUTS = [((16, 256, 256), 'float32')]


def kernel(**inputs):
    import numpy as _np
    import concourse.bacc as _bacc
    from concourse import mybir as _mybir
    from concourse.bass_utils import run_bass_kernel_spmd as _run

    nc = _bacc.Bacc("TRN2", target_bir_lowering=False, num_devices=1)
    arrays, args = {}, []
    for name in _INS:
        a = _np.ascontiguousarray(inputs[name])
        arrays[f"in_{name}_dram"] = a
        args.append(nc.dram_tensor(f"in_{name}_dram", a.shape, _mybir.dt.from_np(a.dtype), kind="ExternalInput").ap())
    for i, (shape, dtype) in enumerate(_OUTS):
        dt = _mybir.dt.from_np(_np.dtype(dtype))
        args.append(nc.dram_tensor(f"out_{i}_dram", shape, dt, kind="ExternalOutput").ap())
    vision_tower_block(nc, *args)
    r = _run(nc, [arrays], core_ids=[0])
    return r.results[0]["out_0_dram"]
```
